# Optimizing a Trainium2 kernel written in Bass

```python
import numpy as np
import jax
import jax.numpy as jnp

def _softmax(x, axis=-1):
    return jax.nn.softmax(x, axis=axis)

def _gelu(x):
    return jax.nn.gelu(x, approximate=True)

def _silu(x):
    return jax.nn.silu(x)

def _sigmoid(x):
    return jax.nn.sigmoid(x)

def _layernorm(x, axis=-1, eps=1e-05):
    m = jnp.mean(x, axis=axis, keepdims=True)
    v = jnp.var(x, axis=axis, keepdims=True)
    return (x - m) / jnp.sqrt(v + eps)

def _scatter_add(tgt, idx, src, axis=0):
    return tgt.at[idx].add(src)

def _segment_sum(src, seg, n):
    return jax.ops.segment_sum(src, seg, n)
kernel_name = 'mk_gnn_preln_d4_gnn_r16_d4883b'

def setup_inputs(seed: int=0):
    np.random.seed(seed)
    _w = jnp.asarray

    def _rec_inputs():
        import jax
        import jax.numpy as jnp
        _gk = jax.random.key(seed)
        x = -8.49e-07 + 0.004471 * jax.random.normal(jax.random.fold_in(_gk, 1), (3125, 64), jnp.float32)
        src = jax.random.randint(jax.random.fold_in(_gk, 2), (100000,), 0, 3125, jnp.int32)
        dst = jax.random.randint(jax.random.fold_in(_gk, 3), (100000,), 0, 3125, jnp.int32)
        _o = jnp.argsort(dst, stable=True)
        src = src[_o]
        dst = dst[_o]
        edge_weight = jax.random.uniform(jax.random.fold_in(_gk, 13), (100000,), jnp.float32, 0.0, 1)
        return (x, src, dst, edge_weight)
    x, src, dst, edge_weight = _rec_inputs()

    def _L0_gnn_setup():
        import jax, jax.numpy as jnp
        import numpy as np
        NUM_NODES = 6250
        EMB_DIM = 64
        N_LAYERS = 3
        N_EDGES = 75000
        key = jax.random.key(seed)
        k_emb, k_edge = jax.random.split(key)
        limit = float(np.sqrt(6.0 / (NUM_NODES + EMB_DIM)))
        emb = jax.random.uniform(k_emb, (NUM_NODES, EMB_DIM), jnp.float32, -limit, limit)
        edge_index = jax.random.randint(k_edge, (2, N_EDGES), 0, NUM_NODES, dtype=jnp.int64)
        return {'emb': emb, 'edge_index': edge_index}
    _L0_gnn_all = _L0_gnn_setup()
    _L0_gnn_in = {k: v for k, v in _L0_gnn_all.items() if k in ()}
    del _L0_gnn_all

    def _L1_gnn_setup():
        import jax, jax.numpy as jnp
        import numpy as np
        N_NODES = 3125
        N_EDGES = 50000
        D_IN = 64
        D_OUT = 64
        key = jax.random.key(seed)
        ks = jax.random.split(key, 8)
        feat = jax.random.normal(ks[0], (N_NODES, D_IN), dtype=jnp.float32)
        weight = jax.random.uniform(ks[1], (N_EDGES,), dtype=jnp.float32)
        W_self = jax.random.normal(ks[2], (D_OUT, D_IN), dtype=jnp.float32) * 0.1
        b_self = jax.random.normal(ks[3], (D_OUT,), dtype=jnp.float32) * 0.1
        W_neigh = jax.random.normal(ks[4], (D_OUT, D_IN), dtype=jnp.float32) * 0.1
        b_neigh = jax.random.normal(ks[5], (D_OUT,), dtype=jnp.float32) * 0.1
        src = jax.random.randint(ks[6], (N_EDGES,), 0, N_NODES, dtype=jnp.int64)
        dst = jax.random.randint(ks[7], (N_EDGES,), 0, N_NODES, dtype=jnp.int64)
        return {'feat': feat, 'weight': weight, 'W_self': W_self, 'b_self': b_self, 'W_neigh': W_neigh, 'b_neigh': b_neigh, 'src': src, 'dst': dst}
    _L1_gnn_all = _L1_gnn_setup()
    _L1_gnn_in = {k: v for k, v in _L1_gnn_all.items() if k in ('W_self', 'b_self', 'W_neigh', 'b_neigh')}
    del _L1_gnn_all

    def _L2_gnn_setup():
        import jax, jax.numpy as jnp
        import numpy as np
        N = 3125
        E = 50000
        C = 64
        K = 3

        def _sym_norm(edge_index, edge_weight, n, lambda_max=2.0):
            src = edge_index[0]
            dst = edge_index[1]
            deg = jax.ops.segment_sum(edge_weight, src, num_segments=n)
            safe = jnp.where(deg > 0, deg, 1.0)
            dis = jnp.where(deg > 0, 1.0 / jnp.sqrt(safe), 0.0)
            w = -dis[src] * edge_weight * dis[dst]
            return 2.0 / lambda_max * w

        def _propagate(x, src, dst, w, n):
            return jax.ops.segment_sum(w[:, None] * x[src], dst, num_segments=n)

        def _cheb_conv(x, src, dst, w, Wk, b, n):
            k_total = Wk.shape[0]
            Tx0 = x
            out = Tx0 @ Wk[0]
            Tx1 = _propagate(Tx0, src, dst, w, n)
            out = out + Tx1 @ Wk[1]
            for k in range(2, k_total):
                Tx2 = 2.0 * _propagate(Tx1, src, dst, w, n) - Tx0
                out = out + Tx2 @ Wk[k]
                Tx0, Tx1 = (Tx1, Tx2)
            return out + b
        key = jax.random.key(seed)
        ks = jax.random.split(key, 16)
        inp = {'X': jax.random.normal(ks[0], (N, C), dtype=jnp.float32), 'edge_index': jax.random.randint(ks[1], (2, E), 0, N, dtype=jnp.int64 if jax.config.jax_enable_x64 else jnp.int32), 'edge_weight': jax.random.uniform(ks[2], (E,), dtype=jnp.float32)}
        names = ['xz', 'hz', 'xr', 'hr', 'xh', 'hh']
        for i, nm in enumerate(names):
            inp['W' + nm] = jax.random.normal(ks[3 + 2 * i], (K, C, C), dtype=jnp.float32) * 0.1
            inp['b' + nm] = jax.random.normal(ks[4 + 2 * i], (C,), dtype=jnp.float32) * 0.1
        return inp
    _L2_gnn_all = _L2_gnn_setup()
    _L2_gnn_in = {k: v for k, v in _L2_gnn_all.items() if k in ('Wxz', 'bxz', 'Whz', 'bhz', 'Wxr', 'bxr', 'Whr', 'bhr', 'Wxh', 'bxh', 'Whh', 'bhh')}
    del _L2_gnn_all

    def _L3_gnn_setup():
        import jax, jax.numpy as jnp
        import numpy as np
        N_NODES = 3125
        N_EDGES = 50000
        EMB = 64
        HEADS = 4
        key = jax.random.key(seed)
        k1, k2, k3, k4, k5, k6 = jax.random.split(key, 6)
        scale = 1.0 / np.sqrt(EMB)
        return {'embeds': jax.random.normal(k1, (N_NODES, EMB), dtype=jnp.float32), 'rows': jax.random.randint(k2, (N_EDGES,), 0, N_NODES, dtype=jnp.int64), 'cols': jax.random.randint(k3, (N_EDGES,), 0, N_NODES, dtype=jnp.int64), 'qTrans': jax.random.normal(k4, (EMB, EMB), dtype=jnp.float32) * scale, 'kTrans': jax.random.normal(k5, (EMB, EMB), dtype=jnp.float32) * scale, 'vTrans': jax.random.normal(k6, (EMB, EMB), dtype=jnp.float32) * scale}
    _L3_gnn_all = _L3_gnn_setup()
    _L3_gnn_in = {k: v for k, v in _L3_gnn_all.items() if k in ('qTrans', 'kTrans', 'vTrans')}
    del _L3_gnn_all
    return {'x': x, 'src': src, 'dst': dst, 'edge_weight': edge_weight, 'L1_gnn_W_self': _L1_gnn_in['W_self'], 'L1_gnn_b_self': _L1_gnn_in['b_self'], 'L1_gnn_W_neigh': _L1_gnn_in['W_neigh'], 'L1_gnn_b_neigh': _L1_gnn_in['b_neigh'], 'L2_gnn_Wxz': _L2_gnn_in['Wxz'], 'L2_gnn_bxz': _L2_gnn_in['bxz'], 'L2_gnn_Whz': _L2_gnn_in['Whz'], 'L2_gnn_bhz': _L2_gnn_in['bhz'], 'L2_gnn_Wxr': _L2_gnn_in['Wxr'], 'L2_gnn_bxr': _L2_gnn_in['bxr'], 'L2_gnn_Whr': _L2_gnn_in['Whr'], 'L2_gnn_bhr': _L2_gnn_in['bhr'], 'L2_gnn_Wxh': _L2_gnn_in['Wxh'], 'L2_gnn_bxh': _L2_gnn_in['bxh'], 'L2_gnn_Whh': _L2_gnn_in['Whh'], 'L2_gnn_bhh': _L2_gnn_in['bhh'], 'L3_gnn_qTrans': _L3_gnn_in['qTrans'], 'L3_gnn_kTrans': _L3_gnn_in['kTrans'], 'L3_gnn_vTrans': _L3_gnn_in['vTrans']}

def reference(x, src, dst, edge_weight, L1_gnn_W_self, L1_gnn_b_self, L1_gnn_W_neigh, L1_gnn_b_neigh, L2_gnn_Wxz, L2_gnn_bxz, L2_gnn_Whz, L2_gnn_bhz, L2_gnn_Wxr, L2_gnn_bxr, L2_gnn_Whr, L2_gnn_bhr, L2_gnn_Wxh, L2_gnn_bxh, L2_gnn_Whh, L2_gnn_bhh, L3_gnn_qTrans, L3_gnn_kTrans, L3_gnn_vTrans):
    import jax
    import jax.numpy as jnp

    def _L0_gnn_ref(emb, edge_index):
        import jax, jax.numpy as jnp
        import numpy as np
        NUM_NODES = 6250
        EMB_DIM = 64
        N_LAYERS = 3
        N_EDGES = 75000
        row, col = (edge_index[0], edge_index[1])
        num_nodes = emb.shape[0]
        ones = jnp.ones(row.shape[0], dtype=emb.dtype)
        deg = jax.ops.segment_sum(ones, col, num_segments=num_nodes)
        deg_inv_sqrt = jnp.where(deg > 0, jax.lax.rsqrt(jnp.maximum(deg, 1.0)), 0.0)
        norm = deg_inv_sqrt[row] * deg_inv_sqrt[col]

        def lgconv(x):
            msgs = x[row] * norm[:, None]
            return jax.ops.segment_sum(msgs, col, num_segments=num_nodes)
        x = emb
        acc = x
        for _ in range(N_LAYERS):
            x = lgconv(x)
            acc = acc + x
        return acc / (N_LAYERS + 1)

    def _L1_gnn_ref(feat, weight, W_self, b_self, W_neigh, b_neigh, src, dst):
        import jax, jax.numpy as jnp
        import numpy as np
        N_NODES = 3125
        N_EDGES = 50000
        D_IN = 64
        D_OUT = 64
        n = feat.shape[0]
        msg = feat[src] * weight[:, None]
        neigh_sum = jax.ops.segment_sum(msg, dst, num_segments=n)
        deg = jax.ops.segment_sum(jnp.ones_like(weight), dst, num_segments=n)
        h_neigh = neigh_sum / jnp.maximum(deg, 1.0)[:, None]
        rst = feat @ W_self.T + b_self + (h_neigh @ W_neigh.T + b_neigh)
        return rst

    def _L2_gnn_ref(X, edge_index, edge_weight, Wxz, bxz, Whz, bhz, Wxr, bxr, Whr, bhr, Wxh, bxh, Whh, bhh):
        import jax, jax.numpy as jnp
        import numpy as np
        N = 3125
        E = 50000
        C = 64
        K = 3

        def _sym_norm(edge_index, edge_weight, n, lambda_max=2.0):
            src = edge_index[0]
            dst = edge_index[1]
            deg = jax.ops.segment_sum(edge_weight, src, num_segments=n)
            safe = jnp.where(deg > 0, deg, 1.0)
            dis = jnp.where(deg > 0, 1.0 / jnp.sqrt(safe), 0.0)
            w = -dis[src] * edge_weight * dis[dst]
            return 2.0 / lambda_max * w

        def _propagate(x, src, dst, w, n):
            return jax.ops.segment_sum(w[:, None] * x[src], dst, num_segments=n)

        def _cheb_conv(x, src, dst, w, Wk, b, n):
            k_total = Wk.shape[0]
            Tx0 = x
            out = Tx0 @ Wk[0]
            Tx1 = _propagate(Tx0, src, dst, w, n)
            out = out + Tx1 @ Wk[1]
            for k in range(2, k_total):
                Tx2 = 2.0 * _propagate(Tx1, src, dst, w, n) - Tx0
                out = out + Tx2 @ Wk[k]
                Tx0, Tx1 = (Tx1, Tx2)
            return out + b
        n = X.shape[0]
        src = edge_index[0]
        dst = edge_index[1]
        w = _sym_norm(edge_index, edge_weight, n)
        H = jnp.zeros((n, Wxz.shape[-1]), dtype=X.dtype)
        Z = jax.nn.sigmoid(_cheb_conv(X, src, dst, w, Wxz, bxz, n) + _cheb_conv(H, src, dst, w, Whz, bhz, n))
        R = jax.nn.sigmoid(_cheb_conv(X, src, dst, w, Wxr, bxr, n) + _cheb_conv(H, src, dst, w, Whr, bhr, n))
        H_tilde = jnp.tanh(_cheb_conv(X, src, dst, w, Wxh, bxh, n) + _cheb_conv(H * R, src, dst, w, Whh, bhh, n))
        return Z * H + (1.0 - Z) * H_tilde

    def _L3_gnn_ref(embeds, rows, cols, qTrans, kTrans, vTrans):
        import jax, jax.numpy as jnp
        import numpy as np
        N_NODES = 3125
        N_EDGES = 50000
        EMB = 64
        HEADS = 4
        n_nodes = embeds.shape[0]
        head_dim = EMB // HEADS
        rowEmb = embeds[rows]
        colEmb = embeds[cols]
        q = (rowEmb @ qTrans).reshape(-1, HEADS, head_dim)
        k = (colEmb @ kTrans).reshape(-1, HEADS, head_dim)
        v = (colEmb @ vTrans).reshape(-1, HEADS, head_dim)
        att = jnp.einsum('ehd,ehd->eh', q, k)
        att = jnp.clip(att, -10.0, 10.0)
        expAtt = jnp.exp(att)
        attNorm = jax.ops.segment_sum(expAtt, rows, num_segments=n_nodes)[rows]
        att = expAtt / (attNorm + 1e-08)
        res = (att[:, :, None] * v).reshape(-1, EMB)
        out = jax.ops.segment_sum(res, rows, num_segments=n_nodes)
        return out
    edge_index = jnp.stack([src, dst])
    h = jnp.maximum(_layernorm(x, axis=-1), 0.0)
    x = x + _L0_gnn_ref(h, edge_index)
    h = jnp.maximum(_layernorm(x, axis=-1), 0.0)
    x = x + _L1_gnn_ref(h, edge_weight, L1_gnn_W_self, L1_gnn_b_self, L1_gnn_W_neigh, L1_gnn_b_neigh, src, dst)
    h = jnp.maximum(_layernorm(x, axis=-1), 0.0)
    x = x + _L2_gnn_ref(h, edge_index, edge_weight, L2_gnn_Wxz, L2_gnn_bxz, L2_gnn_Whz, L2_gnn_bhz, L2_gnn_Wxr, L2_gnn_bxr, L2_gnn_Whr, L2_gnn_bhr, L2_gnn_Wxh, L2_gnn_bxh, L2_gnn_Whh, L2_gnn_bhh)
    h = jnp.maximum(_layernorm(x, axis=-1), 0.0)
    x = x + _L3_gnn_ref(h, src, dst, L3_gnn_qTrans, L3_gnn_kTrans, L3_gnn_vTrans)
    return x

_drawn_inputs = setup_inputs


def setup_inputs(seed=0):
    import zlib

    import numpy as np

    out = dict(_drawn_inputs(seed))
    spreads = {}
    factors = {'L2_gnn_bxz': 3.456, 'L2_gnn_bhz': 3.001}
    for name, (base, spread) in spreads.items():
        noise = np.random.default_rng([zlib.crc32(name.encode()), seed]).standard_normal(out[name].shape)
        drawn = base * np.exp(spread * noise) if base else spread * noise
        out[name] = jnp.asarray(drawn.astype(out[name].dtype))
    for name, factor in factors.items():
        out[name] = (out[name] * factor).astype(out[name].dtype)
    return out
```

```python
from contextlib import ExitStack

import concourse.bass as bass
from concourse import mybir

P = 128
N = 3125
D = 64
E = 100000
HEADS = 4
HD = D // HEADS
T = -(-N // P)
NR = T * P
LAST = N - (T - 1) * P
EC = -(-E // P)
G = 8
GE = G * P
NG = -(-EC // G)
ECP = NG * G
FULL = E // EC
REST = E - FULL * EC
CELLS = NR * NR
PAD_SRC = NR - 1
BANK = 512
CHUNKS = [(c, min(BANK, NR - c)) for c in range(0, NR, BANK)]
PAIRS = T // 2
NPROP = 6
SMALL = 26
EPS = 1e-5
CLIP = 10.0
VW = 32
NPART = 6
QPART = [0, 0, 0, 1, 1, 2]
KPART = [0, 1, 2, 0, 1, 0]

ALU = mybir.AluOpType
ACT = mybir.ActivationFunctionType
AX = mybir.AxisListType
F32 = mybir.dt.float32
BF16 = mybir.dt.bfloat16
I32 = mybir.dt.int32
U32 = mybir.dt.uint32


def gnn_layers(nc, x, src, dst, edge_weight, W_self, b_self, W_neigh, b_neigh,
               Wxz, bxz, bhz, Wxh, bxh, bhh, qTrans, kTrans, vTrans, out):
    with ExitStack() as ctx:
        def sb(name, shape, dt, c=ctx):
            return c.enter_context(nc.sbuf_tensor(name, shape, dt))

        table = nc.dram_tensor("table", [CELLS + GE, 2], F32, kind="Internal").ap()
        keys_dram = nc.dram_tensor("keys_dram", [NG, P * G], F32, kind="Internal").ap()
        weights_dram = nc.dram_tensor("weights_dram", [NR, NR], F32, kind="Internal").ap()
        counts_dram = nc.dram_tensor("counts_dram", [NR, NR], F32, kind="Internal").ap()

        k = {
            "x": sb("x_nodes", [P, T, D], F32),
            "ident": sb("ident", [P, P], F32),
            "fold": sb("fold", [P, D], F32),
            "deg_in": sb("deg_in", [P, T], F32),
            "deg_out": sb("deg_out", [P, T], F32),
            "w_self": sb("w_self", [D + 1, D], F32),
            "w_neigh": sb("w_neigh", [P, D], F32),
            "cheb0": sb("cheb0", [D + 1, 2 * D], F32),
            "cheb1": sb("cheb1", [P, 2 * D], F32),
            "cheb2": sb("cheb2", [P, 2 * D], F32),
            "qk": sb("qk", [D, 2 * D], F32),
            "v": sb("v", [D, D], F32),
        }
        with ExitStack() as c:
            build_table(nc, c, k, sb, table, keys_dram, x, src, dst, edge_weight, W_self, b_self, W_neigh,
                        b_neigh, Wxz, bxz, bhz, Wxh, bxh, bhh, qTrans, kTrans, vTrans)
        with ExitStack() as c:
            split_table(nc, c, k, sb, table, weights_dram, counts_dram)
        with ExitStack() as c:
            propagating_layers(nc, c, k, sb, weights_dram, counts_dram)
        with ExitStack() as c:
            attention_layer(nc, c, k, sb, counts_dram, out)


def build_table(nc, c, k, sb, table, keys_dram, x, src, dst, edge_weight, W_self, b_self, W_neigh, b_neigh,
                Wxz, bxz, bhz, Wxh, bxh, bhh, qTrans, kTrans, vTrans):
    def sem(name):
        return c.enter_context(nc.semaphore(name))

    src_i, dst_i = sb("src_i", [P, ECP], I32, c), sb("dst_i", [P, ECP], I32, c)
    w_e = sb("w_e", [P, ECP], F32, c)
    valid = sb("valid", [P, ECP], F32, c)
    keys = sb("keys", [P, ECP], F32, c)
    keys_rel = sb("keys_rel", [P, ECP], F32, c)
    dummy = sb("dummy_cell", [P, G], F32, c)
    w_rest = sb("w_rest", [P, ECP], F32, c)
    parts = sb("parts", [P, ECP, 10], BF16, c)
    zeros = sb("zeros", [P, 2 * NR], F32, c)
    earlier = sb("earlier", [P, P], BF16, c)
    ones_bf = sb("ones_bf", [P, P], BF16, c)
    ones_f = sb("ones_f", [P, P], F32, c)
    parts_g = sb("parts_g", [P, 2, G, 10], BF16, c)
    key_row = sb("key_row", [P, 2, GE], F32, c)
    equal = [sb(f"equal{b}", [P, G * (GE + 1)], BF16, c) for b in range(2)]
    equal_earlier = sb("equal_earlier", [P, 2, G, P], BF16, c)
    first_rel = sb("first_rel", [P, 2, G], F32, c)
    cell = sb("cell", [P, 2, G], U32, c)
    amount = sb("amount", [P, 2, G, 2], F32, c)
    neigh_in = sb("neigh_in", [D, 2, D], F32, c)
    self_in = sb("self_in", [D, D], F32, c)
    bias_in = sb("bias_in", [D + 1, 3 * D], F32, c)
    cheb2_in = sb("cheb2_in", [D, 2 * D], F32, c)
    totals = c.enter_context(nc.psum_tensor("totals", [P, 2, BANK], F32))
    turned = c.enter_context(nc.psum_tensor("turned", [P, BANK], F32))

    edges_cleared, edges_landed = sem("edges_cleared"), sem("edges_landed")
    zeros_ready, table_zeroed = sem("zeros_ready"), sem("table_zeroed")
    small_cleared, small_landed = sem("small_cleared"), sem("small_landed")
    dve_step, pool_step, turned_copied = sem("dve_step"), sem("pool_step"), sem("turned_copied")
    keys_ready, keys_stored = sem("keys_ready"), sem("keys_stored")
    row_landed = [sem(f"row_landed{b}") for b in range(2)]
    compared, equal_ready = sem("compared"), sem("equal_ready")
    parts_ready, parts_g_ready = sem("parts_ready"), sem("parts_g_ready")
    totals_ready, cells_ready = sem("totals_ready"), sem("cells_ready")
    scattered, group_taken = sem("scattered"), sem("group_taken")
    turned_ready = sem("turned_ready")
    firsts_ready, totals_free = sem("firsts_ready"), sem("totals_free")

    def edge_dmas(sp, tile, dram):
        sp.dma_start(tile[0:FULL, 0:EC], dram[0:FULL * EC].rearrange("(p j) -> p j", j=EC)).then_inc(edges_landed, 16)
        sp.dma_start(tile[FULL:FULL + 1, 0:REST],
                     dram[FULL * EC:E].rearrange("(p j) -> p j", p=1)).then_inc(edges_landed, 16)

    with nc.Block() as block:
        @block.sync
        def _(sp):
            sp.wait_ge(edges_cleared, 3)
            edge_dmas(sp, src_i, src)
            edge_dmas(sp, dst_i, dst)
            edge_dmas(sp, w_e, edge_weight)
            sp.wait_ge(small_cleared, 2)
            small = [(k["x"][:, 0:T - 1, :], x[0:(T - 1) * P].rearrange("(t p) f -> p t f", p=P)),
                     (k["x"][0:LAST, T - 1, :], x[(T - 1) * P:N]),
                     (self_in[:], W_self), (neigh_in[:, 0], W_neigh), (neigh_in[:, 1], W_neigh),
                     (k["qk"][:, 0:D], qTrans), (k["qk"][:, D:2 * D], kTrans), (k["v"][:], vTrans)]
            for g, w in enumerate((Wxz, Wxh)):
                cols = slice(g * D, (g + 1) * D)
                small += [(k["cheb0"][0:D, cols], w[0]), (cheb2_in[:, cols], w[2])]
                for half in range(2):
                    rows = slice(half * D, (half + 1) * D)
                    small += [(k["cheb1"][rows, cols], w[1]), (k["cheb2"][rows, cols], w[2])]
            for to, frm in small:
                sp.dma_start(to, frm).then_inc(small_landed, 16)
            row = slice(D, D + 1)
            for to, frm in ((k["w_self"][row, :], b_self), (bias_in[row, 0:D], b_neigh),
                            (k["cheb0"][row, 0:D], bxz), (bias_in[row, D:2 * D], bhz),
                            (k["cheb0"][row, D:2 * D], bxh), (bias_in[row, 2 * D:3 * D], bhh)):
                sp.dma_start(to, frm.rearrange("(a f) -> a f", a=1)).then_inc(small_landed, 16)
            sp.wait_ge(keys_ready, 1)
            sp.dma_start(keys_dram.rearrange("g (p j) -> p g j", j=G),
                         keys[:].rearrange("p (g j) -> p g j", j=G)).then_inc(keys_stored, 16)
            sp.wait_ge(keys_stored, 16)

            def load_row(g, b):
                sp.dma_start(key_row[:, b, :], keys_dram[bass.ds(g, 1), :].to_broadcast([P, GE])
                             ).then_inc(row_landed[b], 16)

            for b in range(2):
                load_row(b, b)
            with sp.Fori(1, NG // 2) as i:
                for b in range(2):
                    sp.wait_ge(compared, 2 * i - 1 + b)
                    load_row(2 * i + b, b)

        @block.scalar
        def _(act):
            act.wait_ge(zeros_ready, 1)
            cells2 = table[0:CELLS].rearrange("(t p c) two -> t p (c two)", p=P, c=NR)
            with act.Fori(0, T) as t:
                act.dma_start(cells2[bass.ds(t, 1)].rearrange("a p c -> (a p) c"), zeros[:]).then_inc(table_zeroed, 16)
            act.dma_start(table[CELLS:CELLS + GE].rearrange("(p j) two -> p (j two)", p=P),
                          zeros[:, 0:2 * G]).then_inc(table_zeroed, 16)
            act.wait_ge(turned_ready, 1)
            nc.scalar.copy(k["w_neigh"][:], turned[:, 0:D]).then_inc(turned_copied, 1)
            nc.scalar.copy(k["w_self"][0:D, :], turned[0:D, D:2 * D]).then_inc(turned_copied, 1)
            act.wait_ge(parts_ready, 1)

            def take_parts(g, b):
                nc.scalar.copy(parts_g[:, b].rearrange("p j c -> p (j c)"),
                               parts[:].rearrange("p j c -> p (j c)")[:, bass.ds(g * (G * 10), G * 10)]
                               ).then_inc(parts_g_ready, 1)

            for b in range(2):
                take_parts(b, b)
            with act.Fori(1, NG // 2) as i:
                for b in range(2):
                    act.wait_ge(totals_ready, 2 * i - 1 + b)
                    take_parts(2 * i + b, b)

        @block.vector
        def _(dve):
            steps = [0]

            def link(ins):
                steps[0] += 1
                ins.then_inc(dve_step, 1)
                dve.wait_ge(dve_step, steps[0])

            nc.vector.memset(zeros[:], 0.0).then_inc(zeros_ready, 1)
            nc.vector.memset(src_i[:], PAD_SRC).then_inc(edges_cleared, 1)
            nc.vector.memset(dst_i[:], 0).then_inc(edges_cleared, 1)
            nc.vector.memset(w_e[:], 0.0).then_inc(edges_cleared, 1)
            nc.vector.memset(k["x"][:, T - 1, :], 0.0).then_inc(small_cleared, 1)
            nc.vector.memset(ones_bf[:], 1.0).then_inc(small_cleared, 1)
            link(nc.vector.memset(ones_f[:], 1.0))
            link(nc.vector.memset(parts[:, :, 4:5], 1.0))
            link(nc.vector.memset(parts[:, :, 9:10], 0.0))
            dve.wait_ge(edges_landed, 16 * 6)
            link(nc.vector.tensor_scalar(keys[:], src_i[:], float(NR), None, ALU.mult))
            nc.vector.tensor_tensor(keys[:], keys[:], dst_i[:], ALU.add).then_inc(keys_ready, 1)
            dve.wait_ge(keys_ready, 1)
            dve.wait_ge(pool_step, 2)
            link(nc.vector.tensor_tensor(keys_rel[:].rearrange("p (g j) -> p g j", j=G),
                                         keys[:].rearrange("p (g j) -> p g j", j=G),
                                         dummy[:].unsqueeze(1).to_broadcast([P, NG, G]), ALU.subtract))
            link(nc.vector.tensor_copy(parts[:, :, 0], w_e[:]))
            link(nc.vector.tensor_tensor(w_rest[:], w_e[:], parts[:, :, 0], ALU.subtract))
            link(nc.vector.tensor_copy(parts[:, :, 1], w_rest[:]))
            link(nc.vector.tensor_tensor(w_rest[:], w_rest[:], parts[:, :, 1], ALU.subtract))
            link(nc.vector.tensor_copy(parts[:, :, 2], w_rest[:]))
            link(nc.vector.tensor_scalar(parts[:, :, 3], valid[:], float(E), None, ALU.is_lt))
            link(nc.vector.memset(parts[:, EC:ECP, 3:4], 0.0))
            nc.vector.tensor_copy(parts[:, :, 5:9], parts[:, :, 0:4]).then_inc(parts_ready, 1)
            dve.wait_ge(small_landed, 16 * SMALL)
            row = slice(D, D + 1)
            link(nc.vector.tensor_tensor(k["cheb0"][0:D, :], k["cheb0"][0:D, :], cheb2_in[:], ALU.subtract))
            link(nc.vector.tensor_scalar(k["cheb2"][:], k["cheb2"][:], 2.0, None, ALU.mult))
            link(nc.vector.tensor_tensor(k["w_self"][row, :], k["w_self"][row, :], bias_in[row, 0:D], ALU.add))
            link(nc.vector.tensor_tensor(k["cheb0"][row, :], k["cheb0"][row, :], bias_in[row, D:3 * D], ALU.add))

            def compare(g, b, landed):
                dve.wait_ge(row_landed[b], landed)
                for j in range(G):
                    ins = nc.vector.tensor_scalar(equal[b][:, j * GE:(j + 1) * GE], key_row[:, b, :],
                                                  keys[:, bass.ds(g * G + j, 1)], None, ALU.is_equal)
                ins.then_inc(compared, 1)
                dve.wait_ge(compared, g + 1)
                diagonal = equal[b][:].rearrange("p (j r) -> p j r", j=G)[:, :, 0:GE:G]
                nc.vector.tensor_tensor(equal_earlier[:, b], diagonal,
                                        earlier[:].unsqueeze(1).to_broadcast([P, G, P]), ALU.mult
                                        ).then_inc(equal_ready, 1)

            def choose_cells(g, b):
                dve.wait_ge(totals_ready, g + 1)
                sums = totals[:, b, 0:8 * G].rearrange("p (j c) -> p j c", c=8)
                nc.vector.scalar_tensor_tensor(first_rel[:, b], sums[:, :, 4], 0.0, keys_rel[:, bass.ds(g * G, G)],
                                               ALU.is_equal, ALU.mult).then_inc(firsts_ready, 1)
                dve.wait_ge(firsts_ready, g + 1)
                nc.vector.tensor_reduce(amount[:, b, :, 0], sums[:, :, 0:3], AX.X, ALU.add)
                nc.vector.tensor_copy(amount[:, b, :, 1], sums[:, :, 3]).then_inc(totals_free, 1)
                nc.vector.tensor_tensor(cell[:, b], first_rel[:, b], dummy[:], ALU.add).then_inc(cells_ready, 1)

            dve.sem_inc(totals_free, 2)
            dve.wait_ge(pool_step, 3)
            compare(0, 0, 16)
            compare(1, 1, 16)
            choose_cells(0, 0)
            with dve.Fori(1, NG // 2) as i:
                for b in range(2):
                    compare(2 * i + b, b, 16 * i + 16)
                    dve.wait_ge(group_taken, 2 * i - 1 + b)
                    choose_cells(2 * i - 1 + b, 1 - b)
            dve.wait_ge(group_taken, NG - 1)
            choose_cells(NG - 1, 1)

        @block.tensor
        def _(pe):
            pe.wait_ge(small_landed, 16 * SMALL)
            pe.wait_ge(pool_step, 4)
            nc.tensor.transpose(turned[:, 0:D], neigh_in[:].rearrange("p a f -> p (a f)"), k["ident"][0:D, 0:D])
            nc.tensor.transpose(turned[0:D, D:2 * D], self_in[:], k["ident"][0:D, 0:D]).then_inc(turned_ready, 1)
            with pe.Fori(0, NG // 2) as i:
                for b in range(2):
                    g = 2 * i + b
                    pe.wait_ge(totals_free, g + 1)
                    pe.wait_ge(parts_g_ready, g + 1)
                    pe.wait_ge(equal_ready, g + 1)
                    by_column = equal[b][:, 0:G * GE].rearrange("p (j q m) -> p j m q", j=G, m=G)
                    for m in range(G):
                        sums = totals[:, b, 8 * m:8 * m + 5]
                        for j in range(G):
                            flagged = 0 if j < m else 5
                            nc.tensor.matmul(sums, by_column[:, j, m, :], parts_g[:, b, j, flagged:flagged + 5],
                                             start=(j == 0), stop=False, skip_group_check=True)
                        ins = nc.tensor.matmul(sums[:, 4:5], equal_earlier[:, b, m, :], ones_bf[:, 0:1],
                                               start=False, stop=True, skip_group_check=True)
                    ins.then_inc(totals_ready, 1)

        @block.gpsimd
        def _(pool):
            nc.gpsimd.iota(dummy[:], pattern=[[P, G]], base=CELLS, channel_multiplier=1,
                           allow_small_or_imprecise_dtypes=True).then_inc(pool_step, 1)
            nc.gpsimd.iota(valid[:], pattern=[[1, ECP]], base=0, channel_multiplier=EC,
                           allow_small_or_imprecise_dtypes=True).then_inc(pool_step, 1)
            pool.wait_ge(small_cleared, 2)
            nc.gpsimd.affine_select(out=earlier[:], in_=ones_bf[:], compare_op=ALU.is_gt, fill=0.0, base=0,
                                    pattern=[[1, P]], channel_multiplier=-1).then_inc(pool_step, 1)
            pool.wait_ge(dve_step, 1)
            nc.gpsimd.affine_select(out=k["ident"][:], in_=ones_f[:], compare_op=ALU.is_equal, fill=0.0, base=0,
                                    pattern=[[-1, P]], channel_multiplier=1).then_inc(pool_step, 1)
            pool.wait_ge(zeros_ready, 1)
            nc.gpsimd.affine_select(out=k["fold"][:], in_=zeros[:, 0:D], compare_op=ALU.not_equal, fill=1.0, base=0,
                                    pattern=[[-1, D]], channel_multiplier=1).then_inc(pool_step, 1)
            pool.wait_ge(pool_step, 5)
            nc.gpsimd.affine_select(out=k["fold"][:], in_=k["fold"][:], compare_op=ALU.not_equal, fill=1.0, base=-D,
                                    pattern=[[-1, D]], channel_multiplier=1).then_inc(pool_step, 1)
            pool.wait_ge(table_zeroed, 16 * (T + 1))

            def scatter(b):
                for j in range(G):
                    nc.gpsimd.indirect_dma_start(
                        out=table, out_offset=bass.IndirectOffsetOnAxis(ap=cell[:, b, j:j + 1], axis=0),
                        in_=amount[:, b, j, :], in_offset=None, compute_op=ALU.add).then_inc(scattered, 16)

            pool.wait_ge(cells_ready, 1)
            pool.sem_inc(group_taken, 1)
            scatter(0)
            pool.wait_ge(cells_ready, 2)
            pool.wait_ge(scattered, 16 * G)
            pool.sem_inc(group_taken, 1)
            scatter(1)
            with pool.Fori(1, NG // 2) as i:
                for b in range(2):
                    pool.wait_ge(cells_ready, 2 * i + b + 1)
                    pool.wait_ge(scattered, (2 * i + b) * (16 * G))
                    pool.sem_inc(group_taken, 1)
                    scatter(b)
            pool.wait_ge(scattered, 16 * G * NG)


def split_table(nc, c, k, sb, table, weights_dram, counts_dram):
    def sem(name):
        return c.enter_context(nc.semaphore(name))

    cells = sb("cells", [P, 2, NR, 2], F32, c)
    w_tile, c_tile = sb("w_tile", [P, 2, NR], F32, c), sb("c_tile", [P, 2, NR], F32, c)
    ones = sb("ones", [P, 1], F32, c)
    zero_row = sb("zero_row", [1, BANK], BF16, c)
    deg_row = sb("deg_row", [1, NR], F32, c)
    sums = c.enter_context(nc.psum_tensor("deg_sums", [P, 7, BANK], F32))
    nodes = c.enter_context(nc.psum_tensor("deg_nodes", [P, BANK], F32))
    landed = [sem(f"cells_landed{b}") for b in range(2)]
    stored = [sem(f"tiles_stored{b}") for b in range(2)]
    w_split, c_split, ones_set = sem("w_split"), sem("c_split"), sem("ones_set")
    degrees_added, row_copied, turned = sem("degrees_added"), sem("deg_row_copied"), sem("degrees_turned")
    deg_ready = sem("deg_ready")

    with nc.Block() as block:
        @block.sync
        def _(sp):
            rows = table[0:CELLS].rearrange("(t p c) two -> t p (c two)", p=P, c=NR)

            def load(t, b):
                sp.dma_start(cells[:, b].rearrange("p c two -> p (c two)"),
                             rows[bass.ds(t, 1)].rearrange("a p c -> (a p) c")).then_inc(landed[b], 16)

            def store(t, b):
                sp.wait_ge(w_split, t + 1)
                sp.dma_start(weights_dram[bass.ds(t * P, P), :], w_tile[:, b]).then_inc(stored[b], 16)
                sp.wait_ge(c_split, t + 1)
                sp.dma_start(counts_dram[bass.ds(t * P, P), :], c_tile[:, b]).then_inc(stored[b], 16)

            load(0, 0)
            load(1, 1)
            with sp.Fori(0, PAIRS - 1) as i:
                for b in range(2):
                    store(2 * i + b, b)
                    load(2 * i + 2 + b, b)
            store(T - 3, 0)
            load(T - 1, 0)
            store(T - 2, 1)
            store(T - 1, 0)
            sp.wait_ge(stored[0], 32 * (PAIRS + 1))
            sp.wait_ge(stored[1], 32 * PAIRS)

        @block.scalar
        def _(act):
            def split(t, i, b, first):
                act.wait_ge(landed[b], 16 * i + 16)
                if not first:
                    act.wait_ge(stored[b], 32 * i)
                nc.scalar.activation(w_tile[:, b], cells[:, b, :, 0], ACT.Copy,
                                     accum_out=k["deg_out"][:, bass.ds(t, 1)]).then_inc(w_split, 1)

            split(0, 0, 0, True)
            split(1, 0, 1, True)
            with act.Fori(1, PAIRS) as i:
                for b in range(2):
                    split(2 * i + b, i, b, False)
            split(T - 1, PAIRS, 0, False)
            act.wait_ge(degrees_added, T)
            for n, (c0, w) in enumerate(CHUNKS):
                ins = nc.scalar.copy(deg_row[:, c0:c0 + w], sums[0:1, n, 0:w])
            ins.then_inc(row_copied, 1)

        @block.vector
        def _(dve):
            nc.vector.memset(ones[:], 1.0).then_inc(ones_set, 1)
            nc.vector.memset(zero_row[:], 0.0).then_inc(ones_set, 1)

            def split(t, i, b, first):
                dve.wait_ge(landed[b], 16 * i + 16)
                if not first:
                    dve.wait_ge(stored[b], 32 * i)
                    dve.wait_ge(degrees_added, t - 1)
                nc.vector.tensor_copy(c_tile[:, b], cells[:, b, :, 1]).then_inc(c_split, 1)

            split(0, 0, 0, True)
            split(1, 0, 1, True)
            with dve.Fori(1, PAIRS) as i:
                for b in range(2):
                    split(2 * i + b, i, b, False)
            split(T - 1, PAIRS, 0, False)
            dve.wait_ge(turned, 1)
            nc.vector.tensor_copy(k["deg_in"][:], nodes[:, 0:T]).then_inc(deg_ready, 1)
            dve.wait_ge(deg_ready, 1)

        @block.tensor
        def _(pe):
            pe.wait_ge(ones_set, 2)
            for n, (c0, w) in enumerate(CHUNKS):
                nc.tensor.matmul(sums[0:1, n, 0:w], zero_row[:, 0:1], zero_row[:, 0:w], start=True, stop=False,
                                 skip_group_check=True)

            def add_up(t, b):
                pe.wait_ge(c_split, t + 1)
                for n, (c0, w) in enumerate(CHUNKS):
                    ins = nc.tensor.matmul(sums[0:1, n, 0:w], ones[:], c_tile[:, b, c0:c0 + w], start=False,
                                           stop=True, skip_group_check=True)
                ins.then_inc(degrees_added, 1)

            with pe.Fori(0, PAIRS) as i:
                for b in range(2):
                    add_up(2 * i + b, b)
            add_up(T - 1, 0)
            pe.wait_ge(row_copied, 1)
            for t in range(T):
                ins = nc.tensor.matmul(nodes[:, t:t + 1], deg_row[:, t * P:(t + 1) * P], ones[0:1, :], start=True,
                                       stop=True, skip_group_check=True)
            ins.then_inc(turned, 1)


def layer_norm(nc, dve, link, x, h, centred, stat, var_ready, std_ready, layer):
    whole = [P, T, D]
    link(nc.vector.tensor_reduce(stat[:, 0], x[:], AX.X, ALU.add))
    link(nc.vector.tensor_scalar(stat[:, 0], stat[:, 0], 1.0 / D, None, ALU.mult))
    link(nc.vector.tensor_tensor(centred[:], x[:], stat[:, 0].unsqueeze(2).to_broadcast(whole), ALU.subtract))
    link(nc.vector.tensor_tensor(h[:], centred[:], centred[:], ALU.mult))
    link(nc.vector.tensor_reduce(stat[:, 1], h[:], AX.X, ALU.add))
    nc.vector.tensor_scalar(stat[:, 1], stat[:, 1], 1.0 / D, EPS, ALU.mult, ALU.add).then_inc(var_ready, 1)
    dve.wait_ge(std_ready, layer + 1)
    link(nc.vector.reciprocal(stat[:, 0], stat[:, 2]))
    link(nc.vector.tensor_tensor(centred[:], centred[:], stat[:, 0].unsqueeze(2).to_broadcast(whole), ALU.mult))
    link(nc.vector.tensor_scalar(h[:], centred[:], 0.0, None, ALU.max))


def propagating_layers(nc, c, k, sb, weights_dram, counts_dram):
    def sem(name):
        return c.enter_context(nc.semaphore(name))

    x = k["x"]
    h, xs, tmp = sb("h", [P, T, D], F32, c), sb("xs", [P, T, D], F32, c), sb("tmp", [P, T, D], F32, c)
    stat = sb("stat", [P, 3, T], F32, c)
    acc = sb("acc", [P, T, D], F32, c)
    gate = sb("gate", [P, T, 2 * D], F32, c)
    h_t = sb("h_t", [D + 1, NR], F32, c)
    y_t = sb("y_t", [P, 2, NR], F32, c)
    tiles = sb("tiles", [P, 2, 2, NR], F32, c)
    xs_pair = sb("xs_pair", [P, 2, 2, D], F32, c)
    clipped, scale = sb("deg_clipped", [P, 2, T], F32, c), sb("scale", [P, 5, T], F32, c)
    DINV, DIS, NDIS, INV, ROOT = range(5)
    zero_row = sb("zero_row_c", [1, BANK], BF16, c)
    banks = c.enter_context(nc.psum_tensor("banks", [P, 8, BANK], F32))
    flat = banks[:].rearrange("p a b -> p (a b)")

    stages = ["sums0", "nodes0", "sums1", "nodes1", "sums2", "nodes2", "turn1", "sums3", "linear3",
              "turn2", "sums4", "nodes4", "sums5", "gate_neigh", "gate_self"]
    order = {name: n for n, name in enumerate(stages)}
    banks_filled, banks_read = sem("banks_filled"), sem("banks_read")
    consts_set, dve_step = sem("consts_set"), sem("dve_step_c")
    var_ready, std_ready = sem("var_ready"), sem("std_ready")
    deg_ready, root_ready = sem("deg_clipped_ready"), sem("deg_root_ready")
    h_ready, xs_ready = sem("h_ready"), sem("xs_ready")
    gate_ready, gate_done = sem("gate_ready"), sem("gate_done")
    tiles_landed = [sem(f"tiles_landed{b}") for b in range(2)]
    slot_free = [sem(f"slot_free{b}") for b in range(2)]
    pair_ready = [sem(f"pair_ready{b}") for b in range(2)]
    USES = (PAIRS // 2 + 1, PAIRS // 2)

    with nc.Block() as block:
        @block.sync
        def _(sp):
            for prop in range(NPROP):
                matrix = (counts_dram if prop < 3 else weights_dram).rearrange("(t p) d -> p t d", p=P)
                with sp.Fori(0, PAIRS // 2) as i:
                    for b in range(2):
                        sp.wait_ge(slot_free[b], USES[b] * prop + i + 1)
                        sp.dma_start(tiles[:, b], matrix[:, bass.ds(4 * i + 2 * b, 2), :]
                                     ).then_inc(tiles_landed[b], 16)
                sp.wait_ge(slot_free[0], USES[0] * prop + USES[0])
                sp.dma_start(tiles[:, 0, 0], matrix[:, T - 1, :]).then_inc(tiles_landed[0], 16)

        @block.scalar
        def _(act):
            def root(layer):
                act.wait_ge(var_ready, layer + 1)
                nc.scalar.activation(stat[:, 2], stat[:, 1], ACT.Sqrt).then_inc(std_ready, 1)

            def copy_banks(stage, to, rows):
                act.wait_ge(banks_filled, order[stage] + 1)
                for n, (c0, w) in enumerate(CHUNKS):
                    ins = nc.scalar.copy(to[rows, c0:c0 + w], banks[rows, n, 0:w])
                ins.then_inc(banks_read, 1)

            def feed(prop):
                act.wait_ge(xs_ready, prop + 1)
                with act.Fori(0, PAIRS // 2) as i:
                    for b in range(2):
                        act.wait_ge(slot_free[b], USES[b] * prop + i + 1)
                        nc.scalar.copy(xs_pair[:, b], xs[:, bass.ds(4 * i + 2 * b, 2), :]).then_inc(pair_ready[b], 1)
                act.wait_ge(slot_free[0], USES[0] * prop + USES[0])
                nc.scalar.copy(xs_pair[:, 0, 0], xs[:, T - 1, :]).then_inc(pair_ready[0], 1)
                copy_banks(f"sums{prop}", y_t[:, 1 if prop == 5 else 0], slice(0, P))

            act.wait_ge(deg_ready, 1)
            nc.scalar.activation(scale[:, DINV:DIS + 1], clipped[:], ACT.Sqrt).then_inc(root_ready, 1)
            root(0)
            for prop in range(3):
                feed(prop)
            root(1)
            copy_banks("turn1", h_t, slice(0, D))
            feed(3)
            root(2)
            copy_banks("turn2", h_t, slice(0, D))
            feed(4)
            feed(5)
            act.wait_ge(gate_ready, 1)
            nc.scalar.activation(tmp[:], gate[:, :, 0:D], ACT.Sigmoid, scale=-1.0).then_inc(gate_done, 1)
            nc.scalar.activation(h[:], gate[:, :, D:2 * D], ACT.Tanh).then_inc(gate_done, 1)

        @block.vector
        def _(dve):
            steps = [0]

            def link(ins):
                steps[0] += 1
                ins.then_inc(dve_step, 1)
                dve.wait_ge(dve_step, steps[0])

            def nodes_of(stage, width=D, bank=0):
                dve.wait_ge(banks_filled, order[stage] + 1)
                return flat[:, bank * BANK:bank * BANK + T * width].rearrange("p (t f) -> p t f", f=width)

            def per_node(n, width=D):
                return scale[:, n].unsqueeze(2).to_broadcast([P, T, width])

            nc.vector.memset(zero_row[:], 0.0).then_inc(consts_set, 1)
            nc.vector.memset(h_t[D:D + 1, :], 1.0).then_inc(consts_set, 1)
            link(nc.vector.tensor_scalar(scale[:, ROOT], k["deg_out"][:], 0.0, None, ALU.is_gt))
            link(nc.vector.tensor_tensor(clipped[:, 1], k["deg_out"][:], scale[:, ROOT], ALU.mult))
            link(nc.vector.tensor_scalar(scale[:, INV], scale[:, ROOT], -1.0, 1.0, ALU.mult, ALU.add))
            link(nc.vector.tensor_tensor(clipped[:, 1], clipped[:, 1], scale[:, INV], ALU.max))
            nc.vector.tensor_scalar(clipped[:, 0], k["deg_in"][:], 1.0, None, ALU.max).then_inc(deg_ready, 1)
            dve.wait_ge(deg_ready, 1)
            link(nc.vector.reciprocal(scale[:, INV], clipped[:, 0]))
            dve.wait_ge(root_ready, 1)
            link(nc.vector.reciprocal(scale[:, DINV:DIS + 1], scale[:, DINV:DIS + 1]))
            link(nc.vector.tensor_tensor(scale[:, DIS], scale[:, DIS], scale[:, ROOT], ALU.mult))
            link(nc.vector.tensor_scalar(scale[:, NDIS], scale[:, DIS], -1.0, None, ALU.mult))
            link(nc.vector.tensor_scalar(scale[:, ROOT], k["deg_in"][:], 0.0, None, ALU.is_gt))
            link(nc.vector.tensor_tensor(scale[:, DINV], scale[:, DINV], scale[:, ROOT], ALU.mult))

            layer_norm(nc, dve, link, x, h, tmp, stat, var_ready, std_ready, 0)
            nc.vector.tensor_tensor(xs[:], h[:], per_node(DINV), ALU.mult).then_inc(xs_ready, 1)
            for prop in range(3):
                y = nodes_of(f"nodes{prop}")
                nc.vector.tensor_tensor(tmp[:], y, per_node(DINV), ALU.mult).then_inc(banks_read, 1)
                dve.wait_ge(banks_read, order[f"nodes{prop}"] + 1)
                if prop < 2:
                    nc.vector.tensor_tensor(xs[:], tmp[:], per_node(DINV), ALU.mult).then_inc(xs_ready, 1)
                link(nc.vector.tensor_tensor(acc[:], acc[:] if prop else h[:], tmp[:], ALU.add))
            link(nc.vector.scalar_tensor_tensor(x[:], acc[:], 0.25, x[:], ALU.mult, ALU.add))

            layer_norm(nc, dve, link, x, h, tmp, stat, var_ready, std_ready, 1)
            nc.vector.tensor_copy(xs[:], h[:]).then_inc(xs_ready, 1)
            own = nodes_of("linear3", bank=0)
            near = nodes_of("linear3", bank=4)
            link(nc.vector.tensor_tensor(x[:], own, x[:], ALU.add))
            nc.vector.tensor_tensor(tmp[:], near, per_node(INV), ALU.mult).then_inc(banks_read, 1)
            dve.wait_ge(banks_read, order["linear3"] + 1)
            link(nc.vector.tensor_tensor(x[:], x[:], tmp[:], ALU.add))

            layer_norm(nc, dve, link, x, h, tmp, stat, var_ready, std_ready, 2)
            nc.vector.tensor_tensor(xs[:], h[:], per_node(DIS), ALU.mult).then_inc(xs_ready, 1)
            y = nodes_of("nodes4")
            nc.vector.tensor_tensor(tmp[:], y, per_node(DIS), ALU.mult).then_inc(banks_read, 1)
            dve.wait_ge(banks_read, order["nodes4"] + 1)
            nc.vector.tensor_tensor(xs[:], tmp[:], per_node(NDIS), ALU.mult).then_inc(xs_ready, 1)
            near = nodes_of("gate_neigh", 2 * D)
            nc.vector.tensor_tensor(gate[:], near, per_node(NDIS, 2 * D), ALU.mult).then_inc(banks_read, 1)
            own = nodes_of("gate_self", 2 * D)
            dve.wait_ge(banks_read, order["gate_neigh"] + 1)
            nc.vector.tensor_tensor(gate[:], gate[:], own, ALU.add).then_inc(gate_ready, 1)
            dve.wait_ge(gate_done, 2)
            link(nc.vector.tensor_tensor(acc[:], tmp[:], h[:], ALU.mult))
            link(nc.vector.tensor_tensor(x[:], x[:], acc[:], ALU.add))

        @block.tensor
        def _(pe):
            def begin(stage):
                if order[stage]:
                    pe.wait_ge(banks_read, order[stage])

            def product(prop, turn=None):
                begin(f"sums{prop}")
                for n, (c0, w) in enumerate(CHUNKS):
                    nc.tensor.matmul(banks[:, n, 0:w], zero_row[:, 0:P], zero_row[:, 0:w], start=True, stop=False,
                                     skip_group_check=True)
                with pe.Fori(0, PAIRS // 2) as i:
                    for b in range(2):
                        pe.wait_ge(pair_ready[b], USES[b] * prop + i + 1)
                        pe.wait_ge(tiles_landed[b], 16 * USES[b] * prop + 16 * i + 16)
                        for n, (c0, w) in enumerate(CHUNKS):
                            for half in range(2):
                                rows = slice(half * D, half * D + D)
                                ins = nc.tensor.matmul(banks[rows, n, 0:w], xs_pair[:, b, half],
                                                       tiles[:, b, half, c0:c0 + w], start=False, stop=True,
                                                       skip_group_check=True)
                        ins.then_inc(slot_free[b], 1)
                pe.wait_ge(pair_ready[0], USES[0] * prop + USES[0])
                pe.wait_ge(tiles_landed[0], 16 * USES[0] * prop + 16 * USES[0])
                for n, (c0, w) in enumerate(CHUNKS):
                    ins = nc.tensor.matmul(banks[0:D, n, 0:w], xs_pair[:, 0, 0], tiles[:, 0, 0, c0:c0 + w],
                                           start=False, stop=True, skip_group_check=True)
                ins.then_inc(slot_free[0], 1)
                pe.wait_ge(slot_free[0], USES[0] * prop + USES[0] + 1)
                nc.tensor.matmul(banks[0:1, 7, 0:1], zero_row[:, 0:1], zero_row[:, 0:1], start=True, stop=True,
                                 skip_group_check=True).then_inc(banks_filled, 1)

            def by_nodes(stage, terms, width, bank=0, last=True):
                for t in range(T):
                    to = flat[:, bank * BANK + t * width:bank * BANK + (t + 1) * width]
                    for n, (lhs, rhs) in enumerate(terms):
                        ins = nc.tensor.matmul(to, lhs[:, t * P:(t + 1) * P], rhs, start=(n == 0),
                                               stop=(n == len(terms) - 1), skip_group_check=True)
                if last:
                    ins.then_inc(banks_filled, 1)

            def turn(layer, ready):
                begin(f"turn{layer}")
                pe.wait_ge(xs_ready, ready)
                for t in range(T):
                    ins = nc.tensor.transpose(flat[0:D, t * P:(t + 1) * P], h[:, t, :], k["ident"][:])
                ins.then_inc(banks_filled, 1)

            for b in range(2):
                pe.sem_inc(slot_free[b], 1)
            pe.wait_ge(consts_set, 2)
            for prop in range(3):
                product(prop)
                begin(f"nodes{prop}")
                by_nodes(f"nodes{prop}", [(y_t[:, 0], k["fold"][:])], D)
            turn(1, 4)
            product(3)
            begin("linear3")
            by_nodes("linear3", [(h_t, k["w_self"][:])], D, last=False)
            by_nodes("linear3", [(y_t[:, 0], k["w_neigh"][:])], D, bank=4)
            turn(2, 5)
            product(4)
            begin("nodes4")
            by_nodes("nodes4", [(y_t[:, 0], k["fold"][:])], D)
            product(5)
            begin("gate_neigh")
            by_nodes("gate_neigh", [(y_t[:, 0], k["cheb1"][:]), (y_t[:, 1], k["cheb2"][:])], 2 * D)
            begin("gate_self")
            by_nodes("gate_self", [(h_t, k["cheb0"][:])], 2 * D)


def attention_layer(nc, c, k, sb, counts_dram, out):
    def sem(name):
        return c.enter_context(nc.semaphore(name))

    x = k["x"]
    h, tmp = sb("h_d", [P, T, D], F32, c), sb("tmp_d", [P, T, D], F32, c)
    stat = sb("stat_d", [P, 3, T], F32, c)
    h_t = sb("h_t_d", [D, NR], F32, c)
    qk_t = sb("qk_t", [P, NR], F32, c)
    part = sb("qk_part", [P, 3, NR], BF16, c)
    q6, k6 = sb("q6", [NPART * HD, HEADS, NR], BF16, c), sb("k6", [NPART * HD, HEADS, NR], BF16, c)
    v_all = sb("v_all", [P, T, HEADS, VW], F32, c)
    v_tile = sb("v_tile", [P, 2, HEADS * VW], F32, c)
    count = sb("count", [P, 2, 4, P], F32, c)
    e_att = sb("e_att", [P, HEADS, BANK], F32, c)
    p_att = sb("p_att", [P, 2, HEADS, BANK], F32, c)
    o_t = sb("o_t", [P, NR], F32, c)
    den = sb("den", [P, T, HEADS], F32, c)
    zero_row = sb("zero_row_d", [1, BANK], BF16, c)
    banks = c.enter_context(nc.psum_tensor("banks_d", [P, 8, BANK], F32))
    flat = banks[:].rearrange("p a b -> p (a b)")
    scores, count_t, acc = banks[:, 0:4], banks[:, 4:6], banks[:, 6]
    LO, HI = 4.5399929762484854e-05, 22026.465794806718

    dve_step, consts_set = sem("dve_step_d"), sem("consts_set_d")
    var_ready, std_ready = sem("var_ready_d"), sem("std_ready_d")
    h_ready, turned, h_t_ready = sem("h_ready_d"), sem("turned_d"), sem("h_t_ready")
    qk_ready, qk_copied, parts_ready = sem("qk_ready"), sem("qk_copied"), sem("qk_parts_ready")
    v_made, v_copied, rows_placed = sem("v_made"), sem("v_copied"), sem("rows_placed")
    count_landed = [sem(f"count_landed{b}") for b in range(2)]
    count_turned = [sem(f"count_turned{b}") for b in range(2)]
    v_ready = [sem(f"v_ready{b}") for b in range(2)]
    slot_used = [sem(f"slot_used{b}") for b in range(2)]
    v_taken = sem("v_taken")
    scored, expd = [sem(f"scored{f}") for f in range(2)], [sem(f"expd{f}") for f in range(2)]
    clipped, weighted = sem("clipped"), [sem(f"weighted{f}") for f in range(2)]
    acc_read = sem("acc_read")
    nodes_ready, out_ready, out_stored = sem("nodes_ready_d"), sem("out_ready"), sem("out_stored")
    SC = T // 4
    PLACED = 16 * 2 * NPART * HEADS

    def over_tiles(eng, c_reg, body):
        base, n0, n1 = c_reg * T, c_reg * (PAIRS + 1), c_reg * PAIRS
        with eng.Fori(0, PAIRS) as i:
            body(2 * i, 0, n0 + i, base + 2 * i)
            body(2 * i + 1, 1, n1 + i, base + 2 * i + 1)
        body(T - 1, 0, n0 + PAIRS, base + T - 1)

    def over_chunks(eng, chunk):
        with eng.Fori(0, SC) as ci:
            chunk(ci, 4)
        chunk(SC, T - 4 * SC)

    with nc.Block() as block:
        @block.sync
        def _(sp):
            sp.wait_ge(parts_ready, 1)
            for hd in range(HEADS):
                for n in range(NPART):
                    rows = slice(n * HD, (n + 1) * HD)
                    sp.dma_start(q6[rows, hd, :], part[hd * HD:(hd + 1) * HD, QPART[n], :]).then_inc(rows_placed, 16)
                    sp.dma_start(k6[rows, hd, :], part[D + hd * HD:D + (hd + 1) * HD, KPART[n], :]
                                 ).then_inc(rows_placed, 16)
            blocks = counts_dram.rearrange("(s p) d -> p s d", p=P)

            def chunk(ci, width):
                def load(t, b, n, u):
                    sp.wait_ge(count_turned[b], n + 1)
                    sp.dma_start(count[:, b, 0:width], blocks[:, bass.ds(4 * ci, width), bass.ds(t * P, P)]
                                 ).then_inc(count_landed[b], 16)
                over_tiles(sp, ci, load)

            over_chunks(sp, chunk)
            sp.wait_ge(out_ready, 1)
            sp.dma_start(out[0:(T - 1) * P].rearrange("(t p) f -> p t f", p=P), tmp[:, 0:T - 1]).then_inc(out_stored, 16)
            sp.dma_start(out[(T - 1) * P:N], tmp[0:LAST, T - 1]).then_inc(out_stored, 16)
            sp.wait_ge(out_stored, 32)

        @block.scalar
        def _(act):
            act.wait_ge(var_ready, 1)
            nc.scalar.activation(stat[:, 2], stat[:, 1], ACT.Sqrt).then_inc(std_ready, 1)
            act.wait_ge(turned, 1)
            for n, (c0, w) in enumerate(CHUNKS):
                ins = nc.scalar.copy(h_t[:, c0:c0 + w], banks[0:D, n, 0:w])
            ins.then_inc(h_t_ready, 1)
            act.wait_ge(qk_ready, 1)
            for n, (c0, w) in enumerate(CHUNKS):
                ins = nc.scalar.copy(qk_t[:, c0:c0 + w], banks[:, n, 0:w])
            ins.then_inc(qk_copied, 1)

            act.sem_inc(acc_read, 1)
            for f in range(2):
                act.sem_inc(expd[f], 1)

            def chunk(ci, width):
                def exps(t, b, n, u):
                    for f in range(2):
                        two = slice(2 * f, 2 * f + 2)
                        act.wait_ge(scored[f], u + 1)
                        act.wait_ge(weighted[f], u + 1)
                        nc.scalar.activation(e_att[:, two, 0:width * P], scores[:, two, 0:width * P], ACT.Exp
                                             ).then_inc(expd[f], 1)
                over_tiles(act, ci, exps)
                act.wait_ge(slot_used[0], (ci + 1) * (PAIRS + 1) + 1)
                nc.scalar.copy(o_t[:, bass.ds(ci * BANK, width * P)], acc[:, 0:width * P]).then_inc(acc_read, 1)

            over_chunks(act, chunk)

        @block.vector
        def _(dve):
            steps = [0]

            def link(ins):
                steps[0] += 1
                ins.then_inc(dve_step, 1)
                dve.wait_ge(dve_step, steps[0])

            nc.vector.memset(zero_row[:], 0.0).then_inc(consts_set, 1)
            link(nc.vector.memset(v_all[:], 0.0))
            link(nc.vector.memset(v_all[:, :, :, HD:HD + 1], 1.0))
            layer_norm(nc, dve, link, x, h, tmp, stat, var_ready, std_ready, 0)
            dve.sem_inc(h_ready, 1)
            dve.wait_ge(qk_copied, 1)
            link(nc.vector.tensor_copy(part[:, 0], qk_t[:]))
            link(nc.vector.tensor_tensor(qk_t[:], qk_t[:], part[:, 0], ALU.subtract))
            link(nc.vector.tensor_copy(part[:, 1], qk_t[:]))
            link(nc.vector.tensor_tensor(qk_t[:], qk_t[:], part[:, 1], ALU.subtract))
            nc.vector.tensor_copy(part[:, 2], qk_t[:]).then_inc(parts_ready, 1)
            dve.wait_ge(v_made, 1)
            nc.vector.tensor_copy(v_all[:, :, :, 0:HD],
                                  flat[:, 0:T * D].rearrange("p (t h f) -> p t h f", t=T, h=HEADS)).then_inc(v_copied, 1)
            for f in range(2):
                dve.sem_inc(weighted[f], 1)

            def chunk(ci, width):
                def weigh(t, b, n, u):
                    for f in range(2):
                        two = slice(2 * f, 2 * f + 2)
                        e = e_att[:, two, 0:width * P]
                        dve.wait_ge(expd[f], u + 2)
                        nc.vector.tensor_scalar(e, e, HI, LO, ALU.min, ALU.max).then_inc(clipped, 1)
                        if f == 0:
                            dve.wait_ge(count_turned[b], n + 2)
                            dve.wait_ge(slot_used[b], n + 1)
                        dve.wait_ge(clipped, 2 * u + f + 1)
                        nc.vector.tensor_tensor(p_att[:, b, two, 0:width * P], e,
                                                count_t[:, b, 0:width * P].unsqueeze(1).to_broadcast([P, 2, width * P]),
                                                ALU.mult).then_inc(weighted[f], 1)
                over_tiles(dve, ci, weigh)

            over_chunks(dve, chunk)
            dve.wait_ge(nodes_ready, 1)
            o = flat[:, 0:T * P].rearrange("p (t h f) -> p t h f", t=T, h=HEADS)
            link(nc.vector.tensor_scalar(den[:], o[:, :, :, HD], 1e-8, None, ALU.add))
            link(nc.vector.reciprocal(den[:], den[:]))
            link(nc.vector.tensor_tensor(tmp[:].rearrange("p t (h f) -> p (t h) f", h=HEADS),
                                         o[:, :, :, 0:HD].rearrange("p t h f -> p (t h) f"),
                                         den[:].rearrange("p t h -> p (t h)").unsqueeze(2).to_broadcast([P, T * HEADS, HD]),
                                         ALU.mult))
            nc.vector.tensor_tensor(tmp[:], tmp[:], x[:], ALU.add).then_inc(out_ready, 1)

        @block.gpsimd
        def _(pool):
            pool.wait_ge(v_copied, 1)

            def chunk(ci, width):
                def take(t, b, n, u):
                    pool.wait_ge(slot_used[b], n + 1)
                    pool.sem_inc(v_taken, 1)
                    nc.gpsimd.tensor_copy(v_tile[:, b], v_all[:, bass.ds(t, 1)].rearrange("p t h f -> p (t h f)")
                                          ).then_inc(v_ready[b], 1)
                over_tiles(pool, ci, take)

            over_chunks(pool, chunk)

        @block.tensor
        def _(pe):
            pe.wait_ge(h_ready, 1)
            for t in range(T):
                ins = nc.tensor.transpose(flat[0:D, t * P:(t + 1) * P], h[:, t, :], k["ident"][:])
            ins.then_inc(turned, 1)
            pe.wait_ge(h_t_ready, 1)
            for n, (c0, w) in enumerate(CHUNKS):
                ins = nc.tensor.matmul(banks[:, n, 0:w], k["qk"][:], h_t[:, c0:c0 + w], start=True, stop=True)
            ins.then_inc(qk_ready, 1)
            pe.wait_ge(qk_copied, 1)
            for t in range(T):
                ins = nc.tensor.matmul(flat[:, t * D:(t + 1) * D], h_t[:, t * P:(t + 1) * P], k["v"][:], start=True,
                                       stop=True, skip_group_check=True)
            ins.then_inc(v_made, 1)
            pe.wait_ge(v_copied, 1)
            pe.wait_ge(consts_set, 1)
            pe.wait_ge(rows_placed, PLACED)
            for b in range(2):
                pe.sem_inc(count_turned[b], 1)
                pe.sem_inc(slot_used[b], 1)

            def chunk(ci, width):
                W = width * P
                u0, n0, n1 = ci * T, ci * (PAIRS + 1), ci * PAIRS

                def score(t, b, n, u, slot_just_used=False):
                    for hd in range(HEADS):
                        f = hd // 2
                        if hd % 2 == 0:
                            pe.wait_ge(expd[f], u + 1)
                        ins = nc.tensor.matmul(scores[:, hd, 0:W], k6[:, hd, bass.ds(t * P, P)],
                                               q6[:, hd, bass.ds(ci * BANK, W)], start=True, stop=True)
                        if hd % 2:
                            ins.then_inc(scored[f], 1)
                    pe.wait_ge(count_landed[b], 16 * n + 16)
                    if slot_just_used:
                        pe.wait_ge(weighted[1], u + 1)
                    for s in range(width):
                        ins = nc.tensor.transpose(count_t[:, b, s * P:(s + 1) * P], count[:, b, s, :], k["ident"][:])
                    ins.then_inc(count_turned[b], 1)

                def add_values(b, n, u):
                    pe.wait_ge(v_ready[b], n + 1)
                    for f in range(2):
                        pe.wait_ge(weighted[f], u + 2)
                    for hd in range(HEADS):
                        ins = nc.tensor.matmul(acc[hd * VW:(hd + 1) * VW, 0:W], v_tile[:, b, hd * VW:(hd + 1) * VW],
                                               p_att[:, b, hd, 0:W], start=False, stop=True, skip_group_check=True)
                    ins.then_inc(slot_used[b], 1)

                pe.wait_ge(acc_read, ci + 1)
                nc.tensor.matmul(acc[:, 0:W], zero_row[:, 0:P], zero_row[:, 0:W], start=True, stop=False,
                                 skip_group_check=True)
                score(0, 0, n0, u0, slot_just_used=True)
                with pe.Fori(0, PAIRS) as i:
                    score(2 * i + 1, 1, n1 + i, u0 + 2 * i + 1)
                    add_values(0, n0 + i, u0 + 2 * i)
                    score(2 * i + 2, 0, n0 + i + 1, u0 + 2 * i + 2)
                    add_values(1, n1 + i, u0 + 2 * i + 1)
                add_values(0, n0 + PAIRS, u0 + T - 1)

            over_chunks(pe, chunk)
            pe.wait_ge(acc_read, SC + 2)
            for t in range(T):
                ins = nc.tensor.transpose(flat[:, t * P:(t + 1) * P], o_t[:, t * P:(t + 1) * P], k["ident"][:])
            ins.then_inc(nodes_ready, 1)


_INS = ["x", "src", "dst", "edge_weight", "L1_gnn_W_self", "L1_gnn_b_self", "L1_gnn_W_neigh", "L1_gnn_b_neigh",
        "L2_gnn_Wxz", "L2_gnn_bxz", "L2_gnn_bhz", "L2_gnn_Wxh", "L2_gnn_bxh", "L2_gnn_bhh",
        "L3_gnn_qTrans", "L3_gnn_kTrans", "L3_gnn_vTrans"]


def kernel(**inputs):
    import numpy as _np
    import concourse.bacc as _bacc
    from concourse import mybir as _mybir
    from concourse.bass_utils import run_bass_kernel_spmd as _run

    nc = _bacc.Bacc("TRN2", target_bir_lowering=False, num_devices=1)
    arrays, args = {}, []
    for name in _INS:
        a = _np.ascontiguousarray(inputs[name])
        arrays[f"in_{name}_dram"] = a
        args.append(nc.dram_tensor(f"in_{name}_dram", a.shape, _mybir.dt.from_np(a.dtype), kind="ExternalInput").ap())
    args.append(nc.dram_tensor("out_0_dram", (N, D), _mybir.dt.float32, kind="ExternalOutput").ap())
    gnn_layers(nc, *args)
    r = _run(nc, [arrays], core_ids=[0])
    return r.results[0]["out_0_dram"]
```

```python
from contextlib import ExitStack

import concourse.bass as bass
from concourse import mybir

P = 128
N = 3125
D = 64
E = 100000
HEADS = 4
HD = D // HEADS
T = -(-N // P)
NR = T * P
LAST = N - (T - 1) * P
G = 10
GE = G * P
NG = -(-E // GE)
ECP = NG * G
FULL = E // GE
REST = (E - FULL * GE) // G
CELLS = NR * NR
TILE_CELLS = NR * P
LANDED = 16 * G
ZEROED_AHEAD = 4
LOAD_EVERY = 2
LOADS_FROM = T - ZEROED_AHEAD
assert NG % 2 and LOADS_FROM + LOAD_EVERY * (T - 1) <= NG
PAD = NR - 1
BANK = 512
CHUNKS = [(c, min(BANK, NR - c)) for c in range(0, NR, BANK)]
PAIRS = T // 2
NPROP = 6
KEPT = 5
STREAMED = T - KEPT
SMALL = 26
EPS = 1e-5
CLIP = 10.0
RING = 5
VW = 32
NPART = 6
QPART = [0, 0, 0, 1, 1, 2]
KPART = [0, 1, 2, 0, 1, 0]

ALU = mybir.AluOpType
ACT = mybir.ActivationFunctionType
AX = mybir.AxisListType
F32 = mybir.dt.float32
BF16 = mybir.dt.bfloat16
I32 = mybir.dt.int32
U32 = mybir.dt.uint32


def gnn_layers(nc, x, src, dst, edge_weight, W_self, b_self, W_neigh, b_neigh,
               Wxz, bxz, bhz, Wxh, bxh, bhh, qTrans, kTrans, vTrans, out):
    with ExitStack() as ctx:
        def sb(name, shape, dt, c=ctx):
            return c.enter_context(nc.sbuf_tensor(name, shape, dt))

        table = nc.dram_tensor("table", [CELLS + GE, 2], F32, kind="Internal").ap()
        keys_dram = nc.dram_tensor("keys_dram", [NG, P * G], F32, kind="Internal").ap()
        weights_dram = nc.dram_tensor("weights_dram", [NR, NR], F32, kind="Internal").ap()
        counts_dram = nc.dram_tensor("counts_dram", [NR, NR], F32, kind="Internal").ap()

        k = {
            "x": sb("x_nodes", [P, T, D], F32),
            "ident": sb("ident", [P, P], F32),
            "fold": sb("fold", [P, D], F32),
            "deg_in": sb("deg_in", [P, T], F32),
            "deg_out": sb("deg_out", [P, T], F32),
            "w_self": sb("w_self", [D + 1, D], F32),
            "w_neigh": sb("w_neigh", [P, D], F32),
            "cheb0": sb("cheb0", [D + 1, 2 * D], F32),
            "cheb1": sb("cheb1", [P, 2 * D], F32),
            "cheb2": sb("cheb2", [P, 2 * D], F32),
            "qk": sb("qk", [D, 2 * D], F32),
            "v": sb("v", [D, D], F32),
        }
        with ExitStack() as c:
            build_matrices(nc, c, k, sb, table, keys_dram, weights_dram, counts_dram, x, src, dst, edge_weight,
                           W_self, b_self, W_neigh, b_neigh, Wxz, bxz, bhz, Wxh, bxh, bhh, qTrans, kTrans, vTrans)
        with ExitStack() as c:
            propagating_layers(nc, c, k, sb, weights_dram, counts_dram)
        with ExitStack() as c:
            attention_layer(nc, c, k, sb, counts_dram, out)


def build_matrices(nc, c, k, sb, table, keys_dram, weights_dram, counts_dram, x, src, dst, edge_weight,
                   W_self, b_self, W_neigh, b_neigh, Wxz, bxz, bhz, Wxh, bxh, bhh, qTrans, kTrans, vTrans):
    def sem(name):
        return c.enter_context(nc.semaphore(name))

    ZEROS = 2 * NR // 4
    src_i, dst_i = sb("src_i", [P, ECP], I32, c), sb("dst_i", [P, ECP], I32, c)
    w_e = sb("w_e", [P, ECP], F32, c)
    partition = sb("partition", [P, G], F32, c)
    keys = sb("keys", [P, ECP], F32, c)
    keys_rel = sb("keys_rel", [P, 2, G], F32, c)
    dst_tile = sb("dst_tile", [P, ECP], I32, c)
    dummy = sb("dummy_cell", [P, G], F32, c)
    parts = sb("parts", [P, ECP, 10], BF16, c)
    zeros = sb("zeros", [P, ZEROS], F32, c)
    earlier = sb("earlier", [P, P], BF16, c)
    ones_bf = sb("ones_bf", [P, P], BF16, c)
    zero_bf = sb("zero_bf", [1, P], BF16, c)
    ones_f = sb("ones_f", [P, P], F32, c)
    rows_iota, tiles_iota = sb("rows_iota", [P, P], F32, c), sb("tiles_iota", [P, T], F32, c)
    landed_count = sb("landed_count", [P, 1], F32, c)
    extremes = sb("extremes", [P, 2, NG], F32, c)
    group_extremes = sb("group_extremes", [NG, 2], F32, c)
    group_less = sb("group_less", [P, 1], F32, c)
    uses = sb("uses", [NG, 2, T], F32, c)
    tile_uses = sb("tile_uses", [T, 2], F32, c)
    schedule = sb("schedule", [1, 2, T], F32, c)
    load_at = sb("load_at", [1, T + 1], F32, c)
    zeroed_need = sb("zeroed_need", [1, NG], I32, c)
    zero_need, load_need = sb("zero_need", [1, T], I32, c), sb("load_need", [1, T], I32, c)
    store_need = sb("store_need", [1, T], I32, c)
    parts_g = sb("parts_g", [P, 2, G, 10], BF16, c)
    key_row = sb("key_row", [P, 2, GE], F32, c)
    equal = [sb(f"equal{b}", [P, G * (GE + 1)], BF16, c) for b in range(2)]
    equal_earlier = sb("equal_earlier", [P, 2, G, P], BF16, c)
    is_row, is_tile = sb("is_row", [P, 2, G, P], BF16, c), sb("is_tile", [P, 2, G, T], BF16, c)
    first_rel = sb("first_rel", [P, 2, G], F32, c)
    cell = sb("cell", [P, 2, G], U32, c)
    amount = sb("amount", [P, 2, G, 2], F32, c)
    cells = sb("cells", [P, T, P, 2], F32, c)
    w_tile, c_tile = sb("w_tile", [P, 2, T, P], F32, c), sb("c_tile", [P, 2, T, P], F32, c)
    deg_parts = sb("deg_parts", [P, T, T], F32, c)
    neigh_in = sb("neigh_in", [D, 2, D], F32, c)
    self_in = sb("self_in", [D, D], F32, c)
    bias_in = sb("bias_in", [D + 1, 3 * D], F32, c)
    cheb2_in = sb("cheb2_in", [D, 2 * D], F32, c)
    totals = c.enter_context(nc.psum_tensor("totals", [P, 2, BANK], F32))
    turned = c.enter_context(nc.psum_tensor("turned", [P, 2, BANK], F32))
    degrees = c.enter_context(nc.psum_tensor("degrees", [P, BANK], F32))

    edges_cleared, edges_landed = sem("edges_cleared"), sem("edges_landed")
    zeros_ready, dummies_zeroed, tiles_zeroed = sem("zeros_ready"), sem("dummies_zeroed"), sem("tiles_zeroed")
    quarter_zeroed = sem("quarter_zeroed")
    small_cleared, small_landed = sem("small_cleared"), sem("small_landed")
    dve_step, pool_step, turned_copied = sem("dve_step"), sem("pool_step"), sem("turned_copied")
    keys_ready, keys_stored = sem("keys_ready"), sem("keys_stored")
    extremes_ready, extremes_turned = sem("extremes_ready"), sem("extremes_turned")
    needs_ready, group_started = sem("needs_ready"), sem("group_started")
    row_landed = [sem(f"row_landed{b}") for b in range(2)]
    compared, equal_ready = sem("compared"), sem("equal_ready")
    totals_ready, cells_ready = sem("totals_ready"), sem("cells_ready")
    scattered, group_taken = sem("scattered"), sem("group_taken")
    turned_ready = sem("turned_ready")
    firsts_ready, totals_free = sem("firsts_ready"), sem("totals_free")
    cells_landed, w_split, c_split = sem("cells_landed"), sem("w_split"), sem("c_split")
    stored = [sem(f"tiles_stored{b}") for b in range(2)]

    def edge_dmas(sp, tile, dram):
        sp.dma_start(tile[:, 0:FULL * G].rearrange("p (g j) -> p g j", j=G),
                     dram[0:FULL * GE].rearrange("(g p j) -> p g j", p=P, j=G)).then_inc(edges_landed, 16)
        sp.dma_start(tile[0:REST, FULL * G:ECP],
                     dram[FULL * GE:E].rearrange("(p j) -> p j", j=G)).then_inc(edges_landed, 16)

    with nc.Block() as block:
        @block.sync
        def _(sp):
            sp.wait_ge(edges_cleared, 3)
            edge_dmas(sp, src_i, src)
            edge_dmas(sp, dst_i, dst)
            edge_dmas(sp, w_e, edge_weight)
            sp.wait_ge(small_cleared, 3)
            small = [(k["x"][:, 0:T - 1, :], x[0:(T - 1) * P].rearrange("(t p) f -> p t f", p=P)),
                     (k["x"][0:LAST, T - 1, :], x[(T - 1) * P:N]),
                     (self_in[:], W_self), (neigh_in[:, 0], W_neigh), (neigh_in[:, 1], W_neigh),
                     (k["qk"][:, 0:D], qTrans), (k["qk"][:, D:2 * D], kTrans), (k["v"][:], vTrans)]
            for g, w in enumerate((Wxz, Wxh)):
                cols = slice(g * D, (g + 1) * D)
                small += [(k["cheb0"][0:D, cols], w[0]), (cheb2_in[:, cols], w[2])]
                for half in range(2):
                    rows = slice(half * D, (half + 1) * D)
                    small += [(k["cheb1"][rows, cols], w[1]), (k["cheb2"][rows, cols], w[2])]
            for to, frm in small:
                sp.dma_start(to, frm).then_inc(small_landed, 16)
            row = slice(D, D + 1)
            for to, frm in ((k["w_self"][row, :], b_self), (bias_in[row, 0:D], b_neigh),
                            (k["cheb0"][row, 0:D], bxz), (bias_in[row, D:2 * D], bhz),
                            (k["cheb0"][row, D:2 * D], bxh), (bias_in[row, 2 * D:3 * D], bhh)):
                sp.dma_start(to, frm.rearrange("(a f) -> a f", a=1)).then_inc(small_landed, 16)
            sp.wait_ge(keys_ready, 1)
            sp.dma_start(keys_dram.rearrange("g (p j) -> p g j", j=G),
                         keys[:].rearrange("p (g j) -> p g j", j=G)).then_inc(keys_stored, 16)
            sp.wait_ge(keys_stored, 16)

            def load_row(g, b):
                sp.dma_start(key_row[:, b, :], keys_dram[bass.ds(g, 1), :].to_broadcast([P, GE])
                             ).then_inc(row_landed[b], 16)

            for b in range(2):
                load_row(b, b)
            with sp.Fori(1, NG // 2) as i:
                for b in range(2):
                    sp.wait_ge(compared, 2 * i - 1 + b)
                    load_row(2 * i + b, b)
            sp.wait_ge(compared, NG - 2)
            load_row(NG - 1, 0)

        @block.scalar
        def _(act):
            act.wait_ge(zeros_ready, 1)
            blocks = table[0:CELLS].rearrange("(t p c) two -> t p (c two)", p=P, c=NR)
            act.dma_start(table[CELLS:CELLS + GE].rearrange("(p j) two -> p (j two)", p=P),
                          zeros[:, 0:2 * G]).then_inc(dummies_zeroed, 16)

            def zero_tile(t):
                for quarter in range(4):
                    cols = slice(quarter * ZEROS, (quarter + 1) * ZEROS)
                    act.dma_start(blocks[bass.ds(t, 1), :, cols].rearrange("a p c -> (a p) c"), zeros[:]
                                  ).then_inc(quarter_zeroed, 16)
                act.wait_ge(quarter_zeroed, 64 * t + 64)
                act.sem_inc(tiles_zeroed, 1)

            for t in range(2):
                zero_tile(t)
            act.wait_ge(turned_ready, 1)
            nc.scalar.copy(k["w_neigh"][:], turned[:, 0, 0:D]).then_inc(turned_copied, 1)
            nc.scalar.copy(k["w_self"][0:D, :], turned[0:D, 0, D:2 * D]).then_inc(turned_copied, 1)
            act.wait_ge(needs_ready, 4)
            for t in range(2, ZEROED_AHEAD):
                zero_tile(t)
            with act.Fori(ZEROED_AHEAD, T) as t:
                start = act.value_load(zero_need[0:1, bass.ds(t, 1)], min_val=1, max_val=T)
                act.wait_ge(group_started, start)
                zero_tile(t)
            whole = table[0:CELLS].rearrange("(d s p c) two -> d p s (c two)", d=T, p=P, c=P)
            for b in range(2):
                act.sem_inc(stored[b], 32)

            def load(t):
                need = act.value_load(load_need[0:1, bass.ds(t, 1)], min_val=LANDED, max_val=LANDED * NG)
                act.wait_ge(scattered, need)
                act.dma_start(cells[:].rearrange("p s c two -> p s (c two)"),
                              whole[bass.ds(t, 1)].rearrange("a p s c -> (a p) s c")).then_inc(cells_landed, 16)

            def split(t, b, n):
                act.wait_ge(cells_landed, 16 * t + 16)
                act.wait_ge(stored[b], 32 * n + 32)
                for s in range(T):
                    ins = nc.scalar.activation(w_tile[:, b, s], cells[:, s, :, 0], ACT.Copy,
                                               accum_out=deg_parts[:, s, bass.ds(t, 1)])
                ins.then_inc(w_split, 1)
                nc.scalar.copy(c_tile[:, b], cells[:, :, :, 1]).then_inc(c_split, 1)

            def store(t, b):
                start = act.value_load(store_need[0:1, bass.ds(t, 1)], min_val=LANDED, max_val=LANDED * NG)
                act.wait_ge(scattered, start)
                for matrix, tile in ((weights_dram, w_tile), (counts_dram, c_tile)):
                    act.dma_start(matrix.rearrange("(s p) d -> p s d", p=P)[:, :, bass.ds(t * P, P)], tile[:, b]
                                  ).then_inc(stored[b], 16)

            load(0)
            split(0, 0, 0)
            with act.Fori(0, PAIRS) as i:
                for b in range(2):
                    t = 2 * i + b
                    act.wait_ge(w_split, t + 1)
                    act.wait_ge(c_split, t + 1)
                    load(t + 1)
                    store(t, b)
                    split(t + 1, 1 - b, i + b)
            act.wait_ge(w_split, T)
            act.wait_ge(c_split, T)
            store(T - 1, 0)
            act.wait_ge(stored[0], 32 * (PAIRS + 2))
            act.wait_ge(stored[1], 32 * (PAIRS + 1))

        @block.vector
        def _(dve):
            steps = [0]

            def link(ins):
                steps[0] += 1
                ins.then_inc(dve_step, 1)
                dve.wait_ge(dve_step, steps[0])

            nc.vector.memset(src_i[:], PAD).then_inc(edges_cleared, 1)
            nc.vector.memset(dst_i[:], PAD).then_inc(edges_cleared, 1)
            nc.vector.memset(w_e[:], 0.0).then_inc(edges_cleared, 1)
            nc.vector.memset(zeros[:], 0.0).then_inc(zeros_ready, 1)
            nc.vector.memset(k["x"][:, T - 1, :], 0.0).then_inc(small_cleared, 1)
            nc.vector.memset(ones_bf[:], 1.0).then_inc(small_cleared, 1)
            nc.vector.memset(zero_bf[:], 0.0).then_inc(small_cleared, 1)
            link(nc.vector.memset(ones_f[:], 1.0))
            link(nc.vector.memset(parts[:, :, 4:5], 1.0))
            link(nc.vector.memset(parts[:, :, 9:10], 0.0))
            dve.wait_ge(edges_landed, 16 * 6)
            link(nc.vector.tensor_scalar(dst_tile[:], dst_i[:], P.bit_length() - 1, None, ALU.logical_shift_right))
            link(nc.vector.scalar_tensor_tensor(keys[:], src_i[:], float(P), dst_i[:], ALU.mult, ALU.add))
            nc.vector.scalar_tensor_tensor(keys[:], dst_tile[:], float(TILE_CELLS - P), keys[:], ALU.mult, ALU.add
                                           ).then_inc(keys_ready, 1)
            dve.wait_ge(keys_ready, 1)
            link(nc.vector.tensor_scalar(dst_i[:], dst_i[:], P - 1, None, ALU.bitwise_and))
            of_groups = dst_tile[:].rearrange("p (g j) -> p g j", j=G)
            nc.vector.tensor_reduce(extremes[:, 0], of_groups, AX.X, ALU.max)
            nc.vector.tensor_reduce(extremes[:, 1], of_groups, AX.X, ALU.min).then_inc(extremes_ready, 1)
            link(nc.vector.tensor_copy(parts[:, :, 0], w_e[:]))
            link(nc.vector.tensor_tensor(w_e[:], w_e[:], parts[:, :, 0], ALU.subtract))
            link(nc.vector.tensor_copy(parts[:, :, 1], w_e[:]))
            link(nc.vector.tensor_tensor(w_e[:], w_e[:], parts[:, :, 1], ALU.subtract))
            link(nc.vector.tensor_copy(parts[:, :, 2], w_e[:]))
            dve.wait_ge(pool_step, 2)
            link(nc.vector.memset(parts[:, 0:FULL * G, 3:4], 1.0))
            link(nc.vector.tensor_scalar(parts[:, FULL * G:ECP, 3], partition[:], float(REST), None, ALU.is_lt))
            link(nc.vector.tensor_copy(parts[:, :, 5:9], parts[:, :, 0:4]))
            dve.wait_ge(extremes_turned, 1)
            nc.vector.tensor_reduce(group_extremes[:, 0:1], turned[0:NG, 1, 0:P], AX.X, ALU.max)
            link(nc.vector.tensor_reduce(group_extremes[:, 1:2], turned[0:NG, 1, P:2 * P], AX.X, ALU.min))
            dve.wait_ge(pool_step, 8)
            nc.vector.tensor_scalar(uses[:, 1], tiles_iota[0:NG, :], group_extremes[:, 0:1], group_less[0:NG, :],
                                    ALU.is_le, ALU.mult)
            nc.vector.tensor_scalar(uses[:, 0], tiles_iota[0:NG, :], group_extremes[:, 1:2], landed_count[0:NG, :],
                                    ALU.is_ge, ALU.mult).then_inc(extremes_ready, 1)
            dve.wait_ge(extremes_turned, 2)
            nc.vector.tensor_scalar(zeroed_need[:], turned[0:1, 1, 0:NG], 1.0, None, ALU.add).then_inc(needs_ready, 1)
            nc.vector.tensor_reduce(tile_uses[:, 0:1], turned[0:T, 1, P:P + NG], AX.X, ALU.max)
            nc.vector.tensor_reduce(tile_uses[:, 1:2], turned[0:T, 1, 2 * P:2 * P + NG], AX.X, ALU.min
                                    ).then_inc(extremes_ready, 1)
            link(nc.vector.tensor_scalar(schedule[:, 0], tiles_iota[0:1, :], float(LOAD_EVERY * LANDED),
                                         float(LOADS_FROM * LANDED), ALU.mult, ALU.add))
            link(nc.vector.tensor_scalar(schedule[:, 1], tiles_iota[0:1, :], float(1 - ZEROED_AHEAD), None, ALU.add))
            link(nc.vector.memset(load_at[:, T:T + 1], float(NG * LANDED)))
            dve.wait_ge(extremes_turned, 3)
            link(nc.vector.tensor_tensor(load_at[:, 0:T], turned[0:1, 1, 0:T], schedule[:, 0], ALU.max))
            nc.vector.tensor_copy(load_need[:], load_at[:, 0:T]).then_inc(needs_ready, 1)
            nc.vector.tensor_scalar(store_need[:], load_at[:, 1:T + 1], float(LANDED), float(NG * LANDED),
                                    ALU.add, ALU.min).then_inc(needs_ready, 1)
            nc.vector.scalar_tensor_tensor(zero_need[:], turned[0:1, 1, P:P + T], float(NG + 1), schedule[:, 1],
                                           ALU.add, ALU.min).then_inc(needs_ready, 1)

            def compare(g, b, landed):
                dve.wait_ge(row_landed[b], landed)
                for j in range(G):
                    ins = nc.vector.tensor_scalar(equal[b][:, j * GE:(j + 1) * GE], key_row[:, b, :],
                                                  keys[:, bass.ds(g * G + j, 1)], None, ALU.is_equal)
                ins.then_inc(compared, 1)
                edges = bass.ds(g * G, G)
                nc.vector.tensor_copy(parts_g[:, b], parts[:, edges, :])
                nc.vector.tensor_tensor(keys_rel[:, b], keys[:, edges], dummy[:], ALU.subtract)
                nc.vector.tensor_tensor(is_row[:, b], rows_iota[:].unsqueeze(1).to_broadcast([P, G, P]),
                                        dst_i[:, edges].unsqueeze(2).to_broadcast([P, G, P]), ALU.is_equal)
                nc.vector.tensor_tensor(is_tile[:, b], tiles_iota[:].unsqueeze(1).to_broadcast([P, G, T]),
                                        dst_tile[:, edges].unsqueeze(2).to_broadcast([P, G, T]), ALU.is_equal)
                dve.wait_ge(compared, g + 1)
                diagonal = equal[b][:].rearrange("p (j r) -> p j r", j=G)[:, :, 0:GE:G]
                nc.vector.tensor_tensor(equal_earlier[:, b], diagonal,
                                        earlier[:].unsqueeze(1).to_broadcast([P, G, P]), ALU.mult
                                        ).then_inc(equal_ready, 1)

            def choose_cells(g, b):
                dve.wait_ge(totals_ready, g + 1)
                sums = totals[:, b, 0:8 * G].rearrange("p (j c) -> p j c", c=8)
                nc.vector.scalar_tensor_tensor(first_rel[:, b], sums[:, :, 4], 0.0, keys_rel[:, b],
                                               ALU.is_equal, ALU.mult).then_inc(firsts_ready, 1)
                dve.wait_ge(firsts_ready, g + 1)
                nc.vector.tensor_reduce(amount[:, b, :, 0], sums[:, :, 0:3], AX.X, ALU.add)
                nc.vector.tensor_copy(amount[:, b, :, 1], sums[:, :, 3]).then_inc(totals_free, 1)
                nc.vector.tensor_tensor(cell[:, b], first_rel[:, b], dummy[:], ALU.add).then_inc(cells_ready, 1)

            dve.sem_inc(totals_free, 2)
            compare(0, 0, 16)
            compare(1, 1, 16)
            choose_cells(0, 0)
            with dve.Fori(1, NG // 2) as i:
                for b in range(2):
                    compare(2 * i + b, b, 16 * i + 16)
                    dve.wait_ge(group_taken, 2 * i - 1 + b)
                    choose_cells(2 * i - 1 + b, 1 - b)
            compare(NG - 1, 0, 16 * (NG // 2) + 16)
            dve.wait_ge(group_taken, NG - 2)
            choose_cells(NG - 2, 1)
            dve.wait_ge(group_taken, NG - 1)
            choose_cells(NG - 1, 0)
            dve.wait_ge(small_landed, 16 * SMALL)
            row = slice(D, D + 1)
            link(nc.vector.tensor_tensor(k["cheb0"][0:D, :], k["cheb0"][0:D, :], cheb2_in[:], ALU.subtract))
            link(nc.vector.tensor_scalar(k["cheb2"][:], k["cheb2"][:], 2.0, None, ALU.mult))
            link(nc.vector.tensor_tensor(k["w_self"][row, :], k["w_self"][row, :], bias_in[row, 0:D], ALU.add))
            link(nc.vector.tensor_tensor(k["cheb0"][row, :], k["cheb0"][row, :], bias_in[row, D:3 * D], ALU.add))
            link(nc.vector.tensor_copy(k["deg_in"][:], degrees[:, 0:T]))
            dve.wait_ge(w_split, T)
            link(nc.vector.tensor_reduce(k["deg_out"][:], deg_parts[:], AX.X, ALU.add))

        @block.tensor
        def _(pe):
            pe.wait_ge(small_landed, 16 * SMALL)
            pe.wait_ge(pool_step, 4)
            nc.tensor.transpose(turned[:, 0, 0:D], neigh_in[:].rearrange("p a f -> p (a f)"), k["ident"][0:D, 0:D])
            nc.tensor.transpose(turned[0:D, 0, D:2 * D], self_in[:], k["ident"][0:D, 0:D]).then_inc(turned_ready, 1)
            pe.wait_ge(extremes_ready, 1)
            nc.tensor.transpose(turned[0:NG, 1, 0:P], extremes[:, 0], k["ident"][:])
            nc.tensor.transpose(turned[0:NG, 1, P:2 * P], extremes[:, 1], k["ident"][:]).then_inc(extremes_turned, 1)
            pe.wait_ge(extremes_ready, 2)
            nc.tensor.matmul(turned[0:1, 1, 0:NG], group_extremes[:, 0:1], k["ident"][0:NG, 0:NG], start=True, stop=True)
            for n in range(2):
                ins = nc.tensor.transpose(turned[0:T, 1, (n + 1) * P:(n + 1) * P + NG], uses[:, n],
                                          k["ident"][0:NG, 0:NG])
            ins.then_inc(extremes_turned, 1)
            pe.wait_ge(extremes_ready, 3)
            pe.wait_ge(needs_ready, 1)
            for n in range(2):
                ins = nc.tensor.matmul(turned[0:1, 1, n * P:n * P + T], tile_uses[:, n:n + 1], k["ident"][0:T, 0:T],
                                       start=True, stop=True, skip_group_check=True)
            ins.then_inc(extremes_turned, 1)
            nc.tensor.matmul(degrees[:, 0:T], zero_bf[:], zero_bf[:, 0:T], start=True, stop=False, skip_group_check=True)

            def add_up(g, b):
                pe.wait_ge(totals_free, g + 1)
                pe.wait_ge(equal_ready, g + 1)
                by_column = equal[b][:, 0:G * GE].rearrange("p (j q m) -> p j m q", j=G, m=G)
                for m in range(G):
                    sums = totals[:, b, 8 * m:8 * m + 5]
                    for j in range(G):
                        flagged = 0 if j < m else 5
                        nc.tensor.matmul(sums, by_column[:, j, m, :], parts_g[:, b, j, flagged:flagged + 5],
                                         start=(j == 0), stop=False, skip_group_check=True)
                    nc.tensor.matmul(sums[:, 4:5], equal_earlier[:, b, m, :], ones_bf[:, 0:1],
                                     start=False, stop=True, skip_group_check=True)
                for j in range(G):
                    ins = nc.tensor.matmul(degrees[:, 0:T], is_row[:, b, j, :], is_tile[:, b, j, :], start=False,
                                           stop=True, skip_group_check=True)
                ins.then_inc(totals_ready, 1)

            with pe.Fori(0, NG // 2) as i:
                for b in range(2):
                    add_up(2 * i + b, b)
            add_up(NG - 1, 0)

        @block.gpsimd
        def _(pool):
            nc.gpsimd.iota(dummy[:], pattern=[[P, G]], base=CELLS, channel_multiplier=1,
                           allow_small_or_imprecise_dtypes=True).then_inc(pool_step, 1)
            nc.gpsimd.iota(partition[:], pattern=[[0, G]], base=0, channel_multiplier=1,
                           allow_small_or_imprecise_dtypes=True).then_inc(pool_step, 1)
            pool.wait_ge(small_cleared, 3)
            nc.gpsimd.affine_select(out=earlier[:], in_=ones_bf[:], compare_op=ALU.is_gt, fill=0.0, base=0,
                                    pattern=[[1, P]], channel_multiplier=-1).then_inc(pool_step, 1)
            pool.wait_ge(dve_step, 1)
            nc.gpsimd.affine_select(out=k["ident"][:], in_=ones_f[:], compare_op=ALU.is_equal, fill=0.0, base=0,
                                    pattern=[[-1, P]], channel_multiplier=1).then_inc(pool_step, 1)
            nc.gpsimd.iota(rows_iota[:], pattern=[[1, P]], base=0, channel_multiplier=0,
                           allow_small_or_imprecise_dtypes=True).then_inc(pool_step, 1)
            nc.gpsimd.iota(tiles_iota[:], pattern=[[1, T]], base=0, channel_multiplier=0,
                           allow_small_or_imprecise_dtypes=True).then_inc(pool_step, 1)
            nc.gpsimd.iota(landed_count[:], pattern=[[1, 1]], base=LANDED, channel_multiplier=LANDED,
                           allow_small_or_imprecise_dtypes=True).then_inc(pool_step, 1)
            nc.gpsimd.iota(group_less[:], pattern=[[1, 1]], base=-NG, channel_multiplier=1,
                           allow_small_or_imprecise_dtypes=True).then_inc(pool_step, 1)
            pool.wait_ge(zeros_ready, 1)
            nc.gpsimd.affine_select(out=k["fold"][:], in_=zeros[:, 0:D], compare_op=ALU.not_equal, fill=1.0, base=0,
                                    pattern=[[-1, D]], channel_multiplier=1).then_inc(pool_step, 1)
            pool.wait_ge(pool_step, 9)
            nc.gpsimd.affine_select(out=k["fold"][:], in_=k["fold"][:], compare_op=ALU.not_equal, fill=1.0, base=-D,
                                    pattern=[[-1, D]], channel_multiplier=1).then_inc(pool_step, 1)
            pool.wait_ge(needs_ready, 4)
            pool.wait_ge(dummies_zeroed, 16)

            def scatter(g, b):
                pool.sem_inc(group_started, 1)
                need = pool.value_load(zeroed_need[0:1, bass.ds(g, 1)], min_val=1, max_val=T)
                pool.wait_ge(tiles_zeroed, need)
                pool.sem_inc(group_taken, 1)
                for j in range(G):
                    nc.gpsimd.indirect_dma_start(
                        out=table, out_offset=bass.IndirectOffsetOnAxis(ap=cell[:, b, j:j + 1], axis=0),
                        in_=amount[:, b, j, :], in_offset=None, compute_op=ALU.add).then_inc(scattered, 16)

            pool.wait_ge(cells_ready, 1)
            scatter(0, 0)
            pool.wait_ge(cells_ready, 2)
            pool.wait_ge(scattered, LANDED)
            scatter(1, 1)
            with pool.Fori(1, NG // 2) as i:
                for b in range(2):
                    pool.wait_ge(cells_ready, 2 * i + b + 1)
                    pool.wait_ge(scattered, (2 * i + b) * LANDED)
                    scatter(2 * i + b, b)
            pool.wait_ge(cells_ready, NG)
            pool.wait_ge(scattered, (NG - 1) * LANDED)
            scatter(NG - 1, 0)
            pool.wait_ge(scattered, LANDED * NG)


def layer_norm(nc, dve, link, x, h, centred, stat, var_ready, std_ready, layer):
    whole = [P, T, D]
    link(nc.vector.tensor_reduce(stat[:, 0], x[:], AX.X, ALU.add))
    link(nc.vector.tensor_scalar(stat[:, 0], stat[:, 0], 1.0 / D, None, ALU.mult))
    link(nc.vector.tensor_tensor(centred[:], x[:], stat[:, 0].unsqueeze(2).to_broadcast(whole), ALU.subtract))
    link(nc.vector.tensor_tensor(h[:], centred[:], centred[:], ALU.mult))
    link(nc.vector.tensor_reduce(stat[:, 1], h[:], AX.X, ALU.add))
    nc.vector.tensor_scalar(stat[:, 1], stat[:, 1], 1.0 / D, EPS, ALU.mult, ALU.add).then_inc(var_ready, 1)
    dve.wait_ge(std_ready, layer + 1)
    link(nc.vector.reciprocal(stat[:, 0], stat[:, 2]))
    link(nc.vector.tensor_tensor(centred[:], centred[:], stat[:, 0].unsqueeze(2).to_broadcast(whole), ALU.mult))
    link(nc.vector.tensor_scalar(h[:], centred[:], 0.0, None, ALU.max))


def propagating_layers(nc, c, k, sb, weights_dram, counts_dram):
    def sem(name):
        return c.enter_context(nc.semaphore(name))

    x = k["x"]
    h, xs, tmp = sb("h", [P, T, D], F32, c), sb("xs", [P, T, D], F32, c), sb("tmp", [P, T, D], F32, c)
    stat = sb("stat", [P, 3, T], F32, c)
    acc = sb("acc", [P, T, D], F32, c)
    gate = sb("gate", [P, T, 2 * D], F32, c)
    h_t = sb("h_t", [D + 1, NR], F32, c)
    y_t = sb("y_t", [P, 2, NR], F32, c)
    tiles = sb("tiles", [P, 2, 2, NR], F32, c)
    resident = sb("resident", [P, KEPT, NR], F32, c)
    xs_pair = sb("xs_pair", [P, 2, 2, D], F32, c)
    clipped, scale = sb("deg_clipped", [P, 2, T], F32, c), sb("scale", [P, 6, T], F32, c)
    DINV, DIS, NDIS, INV, ROOT, TWICE = range(6)
    zero_row = sb("zero_row_c", [1, BANK], BF16, c)
    banks = c.enter_context(nc.psum_tensor("banks", [P, 8, BANK], F32))
    flat = banks[:].rearrange("p a b -> p (a b)")

    stages = ["sums0", "nodes0", "sums1", "nodes1", "sums2", "nodes2", "turn1", "sums3", "linear3",
              "turn2", "sums4", "nodes4", "sums5", "gate_neigh", "gate_self"]
    order = {name: n for n, name in enumerate(stages)}
    banks_filled, banks_read = sem("banks_filled"), sem("banks_read")
    consts_set, dve_step = sem("consts_set"), sem("dve_step_c")
    var_ready, std_ready = sem("var_ready"), sem("std_ready")
    deg_ready, root_ready = sem("deg_clipped_ready"), sem("deg_root_ready")
    h_ready, xs_ready = sem("h_ready"), sem("xs_ready")
    gate_ready, gate_done = sem("gate_ready"), sem("gate_done")
    tiles_landed = [[sem(f"tiles_landed{b}{f}") for f in range(2)] for b in range(2)]
    slot_free = [[sem(f"slot_free{b}{f}") for f in range(2)] for b in range(2)]
    ENDS = (0, 3, len(CHUNKS))
    pair_ready = [sem(f"pair_ready{b}") for b in range(2)]
    resident_landed, resident_used = sem("resident_landed"), sem("resident_used")
    USES = STREAMED // 4

    with nc.Block() as block:
        @block.sync
        def _(sp):
            for prop in range(NPROP):
                matrix = (counts_dram if prop < 3 else weights_dram).rearrange("(t p) d -> p t d", p=P)
                if prop in (0, 3):
                    if prop:
                        sp.wait_ge(resident_used, prop)
                    sp.dma_start(resident[:], matrix[:, STREAMED:T, :]).then_inc(resident_landed, 16)
                with sp.Fori(0, USES) as i:
                    for b in range(2):
                        for f in range(2):
                            cols = slice(CHUNKS[ENDS[f]][0], sum(CHUNKS[ENDS[f + 1] - 1]))
                            sp.wait_ge(slot_free[b][f], USES * prop + i + 1)
                            sp.dma_start(tiles[:, b, :, cols], matrix[:, bass.ds(4 * i + 2 * b, 2), cols]
                                         ).then_inc(tiles_landed[b][f], 16)

        @block.scalar
        def _(act):
            def root(layer):
                act.wait_ge(var_ready, layer + 1)
                nc.scalar.activation(stat[:, 2], stat[:, 1], ACT.Sqrt).then_inc(std_ready, 1)

            def copy_banks(stage, to, rows):
                act.wait_ge(banks_filled, order[stage] + 1)
                for n, (c0, w) in enumerate(CHUNKS):
                    ins = nc.scalar.copy(to[rows, c0:c0 + w], banks[rows, n, 0:w])
                ins.then_inc(banks_read, 1)

            def feed(prop):
                act.wait_ge(xs_ready, prop + 1)
                with act.Fori(0, USES) as i:
                    for b in range(2):
                        act.wait_ge(slot_free[b][1], USES * prop + i + 1)
                        nc.scalar.copy(xs_pair[:, b], xs[:, bass.ds(4 * i + 2 * b, 2), :]).then_inc(pair_ready[b], 1)
                copy_banks(f"sums{prop}", y_t[:, 1 if prop == 5 else 0], slice(0, P))

            act.wait_ge(deg_ready, 1)
            nc.scalar.activation(scale[:, DINV:DIS + 1], clipped[:], ACT.Sqrt).then_inc(root_ready, 1)
            root(0)
            for prop in range(3):
                feed(prop)
            root(1)
            copy_banks("turn1", h_t, slice(0, D))
            feed(3)
            root(2)
            copy_banks("turn2", h_t, slice(0, D))
            feed(4)
            feed(5)
            act.wait_ge(gate_ready, 1)
            nc.scalar.activation(tmp[:], gate[:, :, 0:D], ACT.Sigmoid, scale=-1.0).then_inc(gate_done, 1)
            nc.scalar.activation(h[:], gate[:, :, D:2 * D], ACT.Tanh).then_inc(gate_done, 1)

        @block.vector
        def _(dve):
            steps = [0]

            def link(ins):
                steps[0] += 1
                ins.then_inc(dve_step, 1)
                dve.wait_ge(dve_step, steps[0])

            def nodes_of(stage, width=D, bank=0):
                dve.wait_ge(banks_filled, order[stage] + 1)
                return flat[:, bank * BANK:bank * BANK + T * width].rearrange("p (t f) -> p t f", f=width)

            def per_node(n, width=D):
                return scale[:, n].unsqueeze(2).to_broadcast([P, T, width])

            nc.vector.memset(zero_row[:], 0.0).then_inc(consts_set, 1)
            nc.vector.memset(h_t[D:D + 1, :], 1.0).then_inc(consts_set, 1)
            link(nc.vector.tensor_scalar(scale[:, ROOT], k["deg_out"][:], 0.0, None, ALU.is_gt))
            link(nc.vector.tensor_tensor(clipped[:, 1], k["deg_out"][:], scale[:, ROOT], ALU.mult))
            link(nc.vector.tensor_scalar(scale[:, INV], scale[:, ROOT], -1.0, 1.0, ALU.mult, ALU.add))
            link(nc.vector.tensor_tensor(clipped[:, 1], clipped[:, 1], scale[:, INV], ALU.max))
            nc.vector.tensor_scalar(clipped[:, 0], k["deg_in"][:], 1.0, None, ALU.max).then_inc(deg_ready, 1)
            dve.wait_ge(deg_ready, 1)
            link(nc.vector.reciprocal(scale[:, INV], clipped[:, 0]))
            dve.wait_ge(root_ready, 1)
            link(nc.vector.reciprocal(scale[:, DINV:DIS + 1], scale[:, DINV:DIS + 1]))
            link(nc.vector.tensor_tensor(scale[:, DIS], scale[:, DIS], scale[:, ROOT], ALU.mult))
            link(nc.vector.tensor_scalar(scale[:, NDIS], scale[:, DIS], -1.0, None, ALU.mult))
            link(nc.vector.tensor_scalar(scale[:, ROOT], k["deg_in"][:], 0.0, None, ALU.is_gt))
            link(nc.vector.tensor_tensor(scale[:, DINV], scale[:, DINV], scale[:, ROOT], ALU.mult))
            link(nc.vector.tensor_tensor(scale[:, TWICE], scale[:, DINV], scale[:, DINV], ALU.mult))

            layer_norm(nc, dve, link, x, h, tmp, stat, var_ready, std_ready, 0)
            nc.vector.tensor_tensor(xs[:], h[:], per_node(DINV), ALU.mult).then_inc(xs_ready, 1)
            for prop in range(3):
                y = nodes_of(f"nodes{prop}")
                if prop < 2:
                    nc.vector.tensor_tensor(xs[:], y, per_node(TWICE), ALU.mult).then_inc(xs_ready, 1)
                nc.vector.tensor_tensor(tmp[:], y, per_node(DINV), ALU.mult).then_inc(banks_read, 1)
                dve.wait_ge(banks_read, order[f"nodes{prop}"] + 1)
                link(nc.vector.tensor_tensor(acc[:], acc[:] if prop else h[:], tmp[:], ALU.add))
            link(nc.vector.scalar_tensor_tensor(x[:], acc[:], 0.25, x[:], ALU.mult, ALU.add))

            layer_norm(nc, dve, link, x, h, tmp, stat, var_ready, std_ready, 1)
            nc.vector.tensor_copy(xs[:], h[:]).then_inc(xs_ready, 1)
            own = nodes_of("linear3", bank=0)
            near = nodes_of("linear3", bank=4)
            link(nc.vector.tensor_tensor(x[:], own, x[:], ALU.add))
            nc.vector.tensor_tensor(tmp[:], near, per_node(INV), ALU.mult).then_inc(banks_read, 1)
            dve.wait_ge(banks_read, order["linear3"] + 1)
            link(nc.vector.tensor_tensor(x[:], x[:], tmp[:], ALU.add))

            layer_norm(nc, dve, link, x, h, tmp, stat, var_ready, std_ready, 2)
            nc.vector.tensor_tensor(xs[:], h[:], per_node(DIS), ALU.mult).then_inc(xs_ready, 1)
            link(nc.vector.tensor_tensor(scale[:, TWICE], scale[:, DIS], scale[:, NDIS], ALU.mult))
            y = nodes_of("nodes4")
            nc.vector.tensor_tensor(xs[:], y, per_node(TWICE), ALU.mult).then_inc(banks_read, 1)
            dve.wait_ge(banks_read, order["nodes4"] + 1)
            dve.sem_inc(xs_ready, 1)
            near = nodes_of("gate_neigh", 2 * D)
            nc.vector.tensor_tensor(gate[:], near, per_node(NDIS, 2 * D), ALU.mult).then_inc(banks_read, 1)
            own = nodes_of("gate_self", 2 * D)
            dve.wait_ge(banks_read, order["gate_neigh"] + 1)
            nc.vector.tensor_tensor(gate[:], gate[:], own, ALU.add).then_inc(gate_ready, 1)
            dve.wait_ge(gate_done, 2)
            link(nc.vector.tensor_tensor(acc[:], tmp[:], h[:], ALU.mult))
            link(nc.vector.tensor_tensor(x[:], x[:], acc[:], ALU.add))

        @block.tensor
        def _(pe):
            def begin(stage):
                if order[stage]:
                    pe.wait_ge(banks_read, order[stage])

            def product(prop, turn=None):
                begin(f"sums{prop}")
                for n, (c0, w) in enumerate(CHUNKS):
                    nc.tensor.matmul(banks[:, n, 0:w], zero_row[:, 0:P], zero_row[:, 0:w], start=True, stop=False,
                                     skip_group_check=True)

                def add(half, n, c0, w, features, tile):
                    return nc.tensor.matmul(banks[half * D:half * D + D, n, 0:w], features, tile[:, c0:c0 + w],
                                            start=False, stop=True, skip_group_check=True)

                def streamed(i):
                    for b in range(2):
                        pe.wait_ge(pair_ready[b], USES * prop + i + 1)
                        for f in range(2):
                            pe.wait_ge(tiles_landed[b][f], 16 * USES * prop + 16 * i + 16)
                            for n in range(ENDS[f], ENDS[f + 1]):
                                for half in range(2):
                                    ins = add(half, n, *CHUNKS[n], xs_pair[:, b, half], tiles[:, b, half])
                            ins.then_inc(slot_free[b][f], 1)

                for t in range(0, KEPT, 2):
                    streamed(t // 2)
                    if t == 0:
                        pe.wait_ge(resident_landed, 16 * (prop // 3 + 1))
                    for n, (c0, w) in enumerate(CHUNKS):
                        for half in range(min(2, KEPT - t)):
                            ins = add(half, n, c0, w, xs[:, STREAMED + t + half], resident[:, t + half])
                ins.then_inc(resident_used, 1)
                with pe.Fori(-(-KEPT // 2), USES) as i:
                    streamed(i)
                pe.wait_ge(slot_free[1][1], USES * prop + USES + 1)
                nc.tensor.matmul(banks[0:1, 7, 0:1], zero_row[:, 0:1], zero_row[:, 0:1], start=True, stop=True,
                                 skip_group_check=True).then_inc(banks_filled, 1)

            def by_nodes(stage, terms, width, bank=0, last=True):
                for t in range(T):
                    to = flat[:, bank * BANK + t * width:bank * BANK + (t + 1) * width]
                    for n, (lhs, rhs) in enumerate(terms):
                        ins = nc.tensor.matmul(to, lhs[:, t * P:(t + 1) * P], rhs, start=(n == 0),
                                               stop=(n == len(terms) - 1), skip_group_check=True)
                if last:
                    ins.then_inc(banks_filled, 1)

            def turn(layer, ready):
                begin(f"turn{layer}")
                pe.wait_ge(xs_ready, ready)
                for t in range(T):
                    ins = nc.tensor.transpose(flat[0:D, t * P:(t + 1) * P], h[:, t, :], k["ident"][:])
                ins.then_inc(banks_filled, 1)

            for b in range(2):
                for f in range(2):
                    pe.sem_inc(slot_free[b][f], 1)
            pe.wait_ge(consts_set, 2)
            for prop in range(3):
                product(prop)
                begin(f"nodes{prop}")
                by_nodes(f"nodes{prop}", [(y_t[:, 0], k["fold"][:])], D)
            turn(1, 4)
            product(3)
            begin("linear3")
            by_nodes("linear3", [(h_t, k["w_self"][:])], D, last=False)
            by_nodes("linear3", [(y_t[:, 0], k["w_neigh"][:])], D, bank=4)
            turn(2, 5)
            product(4)
            begin("nodes4")
            by_nodes("nodes4", [(y_t[:, 0], k["fold"][:])], D)
            product(5)
            begin("gate_neigh")
            by_nodes("gate_neigh", [(y_t[:, 0], k["cheb1"][:]), (y_t[:, 1], k["cheb2"][:])], 2 * D)
            begin("gate_self")
            by_nodes("gate_self", [(h_t, k["cheb0"][:])], 2 * D)


def attention_layer(nc, c, k, sb, counts_dram, out):
    def sem(name):
        return c.enter_context(nc.semaphore(name))

    parts_dram = nc.dram_tensor("parts_dram", [3, 2, HEADS, HD, NR], BF16, kind="Internal").ap()
    x = k["x"]
    h, tmp = sb("h_d", [P, T, D], F32, c), sb("tmp_d", [P, T, D], F32, c)
    stat = sb("stat_d", [P, 3, T], F32, c)
    h_t = sb("h_t_d", [D, NR], F32, c)
    qk_t = sb("qk_t", [P, NR], F32, c)
    part = sb("qk_part", [P, 3, NR], BF16, c)
    q6, k6 = sb("q6", [NPART * HD, HEADS, NR], BF16, c), sb("k6", [NPART * HD, HEADS, NR], BF16, c)
    v_all = sb("v_all", [P, T, HEADS, VW], F32, c)
    v_tile = sb("v_tile", [P, RING, HEADS * VW], F32, c)
    count = sb("count", [P, RING, 4, P], F32, c)
    att = sb("att", [P, RING, HEADS, BANK], F32, c)
    shift = sb("shift", [P, 2], F32, c)
    o_t = sb("o_t", [P, NR], F32, c)
    den = sb("den", [P, T, HEADS], F32, c)
    zero_row = sb("zero_row_d", [1, BANK], BF16, c)
    banks = c.enter_context(nc.psum_tensor("banks_d", [P, 8, BANK], F32))
    flat = banks[:].rearrange("p a b -> p (a b)")
    scores, acc, count_t = banks[:, 0:4], banks[:, 4], [banks[:, n] for n in (5, 6, 7)]
    LO, HI = 4.5399929762484854e-05, 22026.465794806718

    dve_step, consts_set = sem("dve_step_d"), sem("consts_set_d")
    var_ready, std_ready = sem("var_ready_d"), sem("std_ready_d")
    h_ready, turned, h_t_ready = sem("h_ready_d"), sem("turned_d"), sem("h_t_ready")
    qk_ready, qk_copied, parts_ready = sem("qk_ready"), sem("qk_copied"), sem("qk_parts_ready")
    parts_stored, rows_placed = sem("parts_stored"), sem("rows_placed")
    v_made, v_copied = sem("v_made"), sem("v_copied")
    count_landed = [sem(f"count_landed{j}") for j in range(RING)]
    counts_turned, weighted, values_added = sem("counts_turned"), sem("weighted"), sem("values_added")
    scored = [sem(f"scored{f}") for f in range(2)]
    scores_read = [sem(f"scores_read{f}") for f in range(2)]
    expd_high, clipped = sem("expd_high"), sem("clipped")
    acc_full, acc_read = sem("acc_full"), sem("acc_read")
    nodes_ready, out_ready, out_stored = sem("nodes_ready_d"), sem("out_ready"), sem("out_stored")
    SC = T // 4

    USES = T // RING

    def over_tiles(eng, c_reg, body):
        with eng.Fori(0, T // RING) as i:
            for j in range(RING):
                body(RING * i + j, j, c_reg * USES + i, c_reg * T + RING * i + j)

    def over_chunks(eng, chunk):
        with eng.Fori(0, SC) as ci:
            chunk(ci, 4)
        chunk(SC, T - 4 * SC)

    low, high = slice(0, 2), slice(2, 4)
    LOOPED = (T - 2) // RING * RING

    with nc.Block() as block:
        @block.sync
        def _(sp):
            for n in range(3):
                sp.wait_ge(parts_ready, n + 1)
                sp.dma_start(parts_dram[n].rearrange("w h d n -> (w h d) n"), part[:, n]).then_inc(parts_stored, 16)
            sp.wait_ge(parts_stored, 48)
            for n in range(NPART):
                rows = slice(n * HD, (n + 1) * HD)
                sp.dma_start(q6[rows], parts_dram[QPART[n], 0].rearrange("h d n -> d h n")).then_inc(rows_placed, 16)
                sp.dma_start(k6[rows], parts_dram[KPART[n], 1].rearrange("h d n -> d h n")).then_inc(rows_placed, 16)
            blocks = counts_dram.rearrange("(s p) d -> p s d", p=P)

            def chunk(ci, width):
                def load(t, j, n, u):
                    sp.wait_ge(counts_turned, u + 1)
                    sp.dma_start(count[:, j, 0:width], blocks[:, bass.ds(4 * ci, width), bass.ds(t * P, P)]
                                 ).then_inc(count_landed[j], 16)
                over_tiles(sp, ci, load)

            over_chunks(sp, chunk)
            sp.wait_ge(out_ready, 1)
            sp.dma_start(out[0:(T - 1) * P].rearrange("(t p) f -> p t f", p=P), tmp[:, 0:T - 1]).then_inc(out_stored, 16)
            sp.dma_start(out[(T - 1) * P:N], tmp[0:LAST, T - 1]).then_inc(out_stored, 16)
            sp.wait_ge(out_stored, 32)

        @block.scalar
        def _(act):
            act.wait_ge(var_ready, 1)
            nc.scalar.activation(stat[:, 2], stat[:, 1], ACT.Sqrt).then_inc(std_ready, 1)
            act.wait_ge(turned, 1)
            for n, (c0, w) in enumerate(CHUNKS):
                nc.scalar.copy(h_t[:, c0:c0 + w], banks[0:D, n, 0:w]).then_inc(h_t_ready, 1)
            for n, (c0, w) in enumerate(CHUNKS):
                act.wait_ge(qk_ready, n + 1)
                ins = nc.scalar.copy(qk_t[:, c0:c0 + w], banks[:, n, 0:w])
            ins.then_inc(qk_copied, 1)
            act.wait_ge(consts_set, 2)
            nc.scalar.activation(stat[:, 0, 0:1], shift[:, 1:2], ACT.Exp)
            for f in range(2):
                act.sem_inc(scores_read[f], 1)

            def chunk(ci, width):
                W = width * P

                def exps(t, j, n, u):
                    act.wait_ge(values_added, u + 1)
                    act.wait_ge(scored[0], u + 1)
                    nc.scalar.activation(att[:, j, low, 0:W], scores[:, low, 0:W], ACT.Exp).then_inc(scores_read[0], 1)
                    act.wait_ge(scored[1], u + 1)
                    nc.scalar.activation(att[:, j, high, 0:W], scores[:, high, 0:W], ACT.Relu, bias=shift[:, 0:1]
                                         ).then_inc(scores_read[1], 1)
                    act.wait_ge(scores_read[1], u + 2)
                    nc.scalar.activation(att[:, j, high, 0:W], att[:, j, high, 0:W], ACT.Exp, bias=shift[:, 1:2]
                                         ).then_inc(expd_high, 1)
                over_tiles(act, ci, exps)

            over_chunks(act, chunk)

        @block.vector
        def _(dve):
            steps = [0]

            def link(ins):
                steps[0] += 1
                ins.then_inc(dve_step, 1)
                dve.wait_ge(dve_step, steps[0])

            layer_norm(nc, dve, link, x, h, tmp, stat, var_ready, std_ready, 0)
            dve.sem_inc(h_ready, 1)
            nc.vector.memset(zero_row[:], 0.0).then_inc(consts_set, 1)
            nc.vector.memset(shift[:, 0:1], CLIP)
            nc.vector.memset(shift[:, 1:2], -CLIP).then_inc(consts_set, 1)
            link(nc.vector.memset(v_all[:], 0.0))
            nc.vector.memset(v_all[:, :, :, HD:HD + 1], 1.0)
            dve.wait_ge(v_made, 1)
            nc.vector.tensor_copy(v_all[:, :, :, 0:HD],
                                  flat[:, 0:T * D].rearrange("p (t h f) -> p t h f", t=T, h=HEADS)).then_inc(v_copied, 1)
            dve.wait_ge(qk_copied, 1)
            for n in range(3):
                nc.vector.tensor_copy(part[:, n], qk_t[:]).then_inc(parts_ready, 1)
                dve.wait_ge(parts_ready, n + 1)
                if n < 2:
                    link(nc.vector.tensor_tensor(qk_t[:], qk_t[:], part[:, n], ALU.subtract))
            dve.sem_inc(weighted, 2)
            dve.sem_inc(acc_read, 1)

            def chunk(ci, width):
                W = width * P

                def weigh(t, j, n, u):
                    dve.wait_ge(scores_read[0], u + 2)
                    nc.vector.tensor_scalar(att[:, j, low, 0:W], att[:, j, low, 0:W], HI, LO, ALU.min, ALU.max
                                            ).then_inc(clipped, 1)
                    nc.vector.tensor_copy(v_tile[:, j], v_all[:, bass.ds(t, 1)].rearrange("p a h f -> p (a h f)"))
                    dve.wait_ge(counts_turned, u + RING + 1)
                    dve.wait_ge(clipped, u + 1)
                    times = count_t[j % 3][:, 0:W].unsqueeze(1).to_broadcast([P, 2, W])
                    nc.vector.tensor_tensor(att[:, j, low, 0:W], att[:, j, low, 0:W], times, ALU.mult)
                    dve.wait_ge(expd_high, u + 1)
                    nc.vector.scalar_tensor_tensor(att[:, j, high, 0:W], att[:, j, high, 0:W], HI, times,
                                                   ALU.min, ALU.mult).then_inc(weighted, 1)
                over_tiles(dve, ci, weigh)
                dve.wait_ge(acc_full, ci + 1)
                nc.vector.tensor_copy(o_t[:, bass.ds(ci * BANK, W)], acc[:, 0:W]).then_inc(acc_read, 1)

            over_chunks(dve, chunk)
            dve.wait_ge(nodes_ready, 1)
            o = flat[:, 0:T * P].rearrange("p (t h f) -> p t h f", t=T, h=HEADS)
            link(nc.vector.tensor_scalar(den[:], o[:, :, :, HD], 1e-8, None, ALU.add))
            link(nc.vector.reciprocal(den[:], den[:]))
            link(nc.vector.tensor_tensor(tmp[:].rearrange("p t (h f) -> p (t h) f", h=HEADS),
                                         o[:, :, :, 0:HD].rearrange("p t h f -> p (t h) f"),
                                         den[:].rearrange("p t h -> p (t h)").unsqueeze(2).to_broadcast([P, T * HEADS, HD]),
                                         ALU.mult))
            nc.vector.tensor_tensor(tmp[:], tmp[:], x[:], ALU.add).then_inc(out_ready, 1)

        @block.tensor
        def _(pe):
            pe.wait_ge(h_ready, 1)
            for t in range(T):
                ins = nc.tensor.transpose(flat[0:D, t * P:(t + 1) * P], h[:, t, :], k["ident"][:])
            ins.then_inc(turned, 1)
            for n, (c0, w) in enumerate(CHUNKS):
                pe.wait_ge(h_t_ready, n + 1)
                nc.tensor.matmul(banks[:, n, 0:w], k["qk"][:], h_t[:, c0:c0 + w], start=True, stop=True
                                 ).then_inc(qk_ready, 1)
            pe.wait_ge(qk_copied, 1)
            for t in range(T):
                ins = nc.tensor.matmul(flat[:, t * D:(t + 1) * D], h_t[:, t * P:(t + 1) * P], k["v"][:], start=True,
                                       stop=True, skip_group_check=True)
            ins.then_inc(v_made, 1)
            pe.wait_ge(v_copied, 1)
            pe.wait_ge(consts_set, 2)
            pe.wait_ge(rows_placed, 16 * 2 * NPART)
            pe.sem_inc(counts_turned, RING)
            pe.sem_inc(values_added, RING)

            def chunk(ci, width):
                W = width * P

                def score(t, j, n, u):
                    for hd in range(HEADS):
                        f = hd // 2
                        if hd % 2 == 0:
                            pe.wait_ge(scores_read[f], u + 1)
                        ins = nc.tensor.matmul(scores[:, hd, 0:W], k6[:, hd, bass.ds(t * P, P)],
                                               q6[:, hd, bass.ds(ci * BANK, W)], start=True, stop=True)
                        if hd % 2:
                            ins.then_inc(scored[f], 1)
                    pe.wait_ge(count_landed[j], 16 * n + 16)
                    pe.wait_ge(weighted, u + 1)
                    for s in range(width):
                        ins = nc.tensor.transpose(count_t[j % 3][:, s * P:(s + 1) * P], count[:, j, s, :], k["ident"][:])
                    ins.then_inc(counts_turned, 1)

                def add_values(j, u, last=False):
                    pe.wait_ge(weighted, u + 3)
                    for hd in range(HEADS):
                        ins = nc.tensor.matmul(acc[hd * VW:(hd + 1) * VW, 0:W], v_tile[:, j, hd * VW:(hd + 1) * VW],
                                               att[:, j, hd, 0:W], start=False, stop=True, skip_group_check=True)
                    ins.then_inc(values_added, 1)

                def step(t, j, n):
                    score(t, j, ci * USES + n, ci * T + t)
                    add_values((j - 2) % RING, ci * T + t - 2)

                for t in range(2):
                    score(t, t, ci * USES, ci * T + t)
                pe.wait_ge(acc_read, ci + 1)
                nc.tensor.matmul(acc[:, 0:W], zero_row[:, 0:P], zero_row[:, 0:W], start=True, stop=False,
                                 skip_group_check=True)
                with pe.Fori(0, LOOPED // RING) as i:
                    for s in range(RING):
                        step(RING * i + 2 + s, (2 + s) % RING, i + (2 + s) // RING)
                for t in range(2 + LOOPED, T):
                    step(t, t % RING, t // RING)
                for t in range(T - 2, T):
                    add_values(t % RING, ci * T + t)
                pe.wait_ge(values_added, ci * T + T + RING)
                pe.sem_inc(acc_full, 1)

            over_chunks(pe, chunk)
            pe.wait_ge(acc_read, SC + 2)
            for t in range(T):
                ins = nc.tensor.transpose(flat[:, t * P:(t + 1) * P], o_t[:, t * P:(t + 1) * P], k["ident"][:])
            ins.then_inc(nodes_ready, 1)


_INS = ["x", "src", "dst", "edge_weight", "L1_gnn_W_self", "L1_gnn_b_self", "L1_gnn_W_neigh", "L1_gnn_b_neigh",
        "L2_gnn_Wxz", "L2_gnn_bxz", "L2_gnn_bhz", "L2_gnn_Wxh", "L2_gnn_bxh", "L2_gnn_bhh",
        "L3_gnn_qTrans", "L3_gnn_kTrans", "L3_gnn_vTrans"]


def kernel(**inputs):
    import numpy as _np
    import concourse.bacc as _bacc
    from concourse import mybir as _mybir
    from concourse.bass_utils import run_bass_kernel_spmd as _run

    nc = _bacc.Bacc("TRN2", target_bir_lowering=False, num_devices=1)
    arrays, args = {}, []
    for name in _INS:
        a = _np.ascontiguousarray(inputs[name])
        arrays[f"in_{name}_dram"] = a
        args.append(nc.dram_tensor(f"in_{name}_dram", a.shape, _mybir.dt.from_np(a.dtype), kind="ExternalInput").ap())
    args.append(nc.dram_tensor("out_0_dram", (N, D), _mybir.dt.float32, kind="ExternalOutput").ap())
    gnn_layers(nc, *args)
    r = _run(nc, [arrays], core_ids=[0])
    return r.results[0]["out_0_dram"]
```

```python
from contextlib import ExitStack

import concourse.bass as bass
from concourse import mybir

P = 128
N = 3125
D = 64
E = 100000
HEADS = 4
HD = D // HEADS
T = -(-N // P)
NR = T * P
LAST = N - (T - 1) * P
G = 10
GE = G * P
NG = -(-E // GE)
ECP = NG * G
FULL = E // GE
REST = (E - FULL * GE) // G
CELLS = NR * NR
TILE_CELLS = NR * P
LANDED = 16 * G
ZEROED_AHEAD = 2
LOAD_EVERY = 2
LOADS_FROM = T - ZEROED_AHEAD
assert NG % 2 and LOADS_FROM + LOAD_EVERY * (T - 1) <= NG
PAD = NR - 1
BANK = 512
CHUNKS = [(c, min(BANK, NR - c)) for c in range(0, NR, BANK)]
PAIRS = T // 2
NPROP = 6
KEPT = 7
STREAMED = T - KEPT
SMALL = 26
EPS = 1e-5
CLIP = 10.0
RING = 5
VW = 32
NPART = 6
QPART = [0, 0, 0, 1, 1, 2]
KPART = [0, 1, 2, 0, 1, 0]

ALU = mybir.AluOpType
ACT = mybir.ActivationFunctionType
AX = mybir.AxisListType
F32 = mybir.dt.float32
BF16 = mybir.dt.bfloat16
I32 = mybir.dt.int32
U32 = mybir.dt.uint32


def gnn_layers(nc, x, src, dst, edge_weight, W_self, b_self, W_neigh, b_neigh,
               Wxz, bxz, bhz, Wxh, bxh, bhh, qTrans, kTrans, vTrans, out):
    with ExitStack() as ctx:
        def sb(name, shape, dt, c=ctx):
            return c.enter_context(nc.sbuf_tensor(name, shape, dt))

        table = nc.dram_tensor("table", [CELLS + GE, 2], F32, kind="Internal").ap()
        keys_dram = nc.dram_tensor("keys_dram", [NG, P * G], F32, kind="Internal").ap()
        weights_dram = nc.dram_tensor("weights_dram", [NR, NR], F32, kind="Internal").ap()
        counts_dram = nc.dram_tensor("counts_dram", [NR, NR], F32, kind="Internal").ap()

        k = {
            "x": sb("x_nodes", [P, T, D], F32),
            "h": sb("h", [P, T, D], F32),
            "stat": sb("stat", [P, 3, T], F32),
            "ident": sb("ident", [P, P], F32),
            "deg_in": sb("deg_in", [P, T], F32),
            "deg_out": sb("deg_out", [P, T], F32),
            "w_self": sb("w_self", [D + 1, D], F32),
            "w_neigh": sb("w_neigh", [P, D], F32),
            "cheb0": sb("cheb0", [D + 1, 2 * D], F32),
            "cheb1": sb("cheb1", [P, 2 * D], F32),
            "cheb2": sb("cheb2", [P, 2 * D], F32),
            "qk": sb("qk", [D, 2 * D], F32),
            "v": sb("v", [D, D], F32),
        }
        with ExitStack() as c:
            build_matrices(nc, c, k, sb, table, keys_dram, weights_dram, counts_dram, x, src, dst, edge_weight,
                           W_self, b_self, W_neigh, b_neigh, Wxz, bxz, bhz, Wxh, bxh, bhh, qTrans, kTrans, vTrans)
        with ExitStack() as c:
            propagating_layers(nc, c, k, sb, weights_dram, counts_dram)
        with ExitStack() as c:
            attention_layer(nc, c, k, sb, counts_dram, out)


def build_matrices(nc, c, k, sb, table, keys_dram, weights_dram, counts_dram, x, src, dst, edge_weight,
                   W_self, b_self, W_neigh, b_neigh, Wxz, bxz, bhz, Wxh, bxh, bhh, qTrans, kTrans, vTrans):
    def sem(name):
        return c.enter_context(nc.semaphore(name))

    ZEROS = 2 * NR // 4
    src_i, dst_i = sb("src_i", [P, ECP], I32, c), sb("dst_i", [P, ECP], I32, c)
    w_e = sb("w_e", [P, ECP], F32, c)
    partition = sb("partition", [P, G], F32, c)
    keys = sb("keys", [P, ECP], F32, c)
    keys_rel = sb("keys_rel", [P, 2, G], F32, c)
    dst_tile = sb("dst_tile", [P, ECP], I32, c)
    dummy = sb("dummy_cell", [P, G], F32, c)
    parts = sb("parts", [P, ECP, 5], BF16, c)
    zeros = sb("zeros", [P, ZEROS], F32, c)
    earlier = sb("earlier", [P, P], BF16, c)
    ones_bf = sb("ones_bf", [P, P], BF16, c)
    zero_bf = sb("zero_bf", [1, P], BF16, c)
    ones_f = sb("ones_f", [P, P], F32, c)
    rows_iota, tiles_iota = sb("rows_iota", [P, P], F32, c), sb("tiles_iota", [P, T], F32, c)
    landed_count = sb("landed_count", [P, 1], F32, c)
    extremes = sb("extremes", [P, 2, NG], F32, c)
    group_extremes = sb("group_extremes", [NG, 2], F32, c)
    group_less = sb("group_less", [P, 1], F32, c)
    uses = sb("uses", [NG, 2, T], F32, c)
    tile_uses = sb("tile_uses", [T, 2], F32, c)
    schedule = sb("schedule", [1, 2, T], F32, c)
    load_at = sb("load_at", [1, T + 1], F32, c)
    zeroed_need = sb("zeroed_need", [1, NG], I32, c)
    zero_need, load_need = sb("zero_need", [1, T], I32, c), sb("load_need", [1, T], I32, c)
    store_need = sb("store_need", [1, T], I32, c)
    parts_g = sb("parts_g", [P, 2, G, 5], BF16, c)
    key_row = sb("key_row", [P, 2, GE], F32, c)
    equal = [sb(f"equal{b}", [P, G * (GE + 1)], BF16, c) for b in range(2)]
    equal_earlier = sb("equal_earlier", [P, 2, G, P], BF16, c)
    is_row, is_tile = sb("is_row", [P, 2, G, P], BF16, c), sb("is_tile", [P, 2, G, T], BF16, c)
    first_rel = sb("first_rel", [P, 2, G], F32, c)
    cell = sb("cell", [P, 2, G], U32, c)
    amount = sb("amount", [P, 2, G, 2], F32, c)
    cells = sb("cells", [P, T, P, 2], F32, c)
    w_tile, c_tile = sb("w_tile", [P, 2, T, P], F32, c), sb("c_tile", [P, 2, T, P], F32, c)
    deg_parts = sb("deg_parts", [P, T, T], F32, c)
    neigh_in = sb("neigh_in", [D, 2, D], F32, c)
    self_in = sb("self_in", [D, D], F32, c)
    bias_in = sb("bias_in", [D + 1, 3 * D], F32, c)
    cheb2_in = sb("cheb2_in", [D, 2 * D], F32, c)
    totals = c.enter_context(nc.psum_tensor("totals", [P, 2, BANK], F32))
    turned = c.enter_context(nc.psum_tensor("turned", [P, 2, BANK], F32))
    centred = key_row[:].rearrange("p b r -> p (b r)")[:, 0:T * D].rearrange("p (t f) -> p t f", f=D)
    degrees = c.enter_context(nc.psum_tensor("degrees", [P, BANK], F32))

    edges_cleared, edges_landed = sem("edges_cleared"), sem("edges_landed")
    weights_landed = sem("weights_landed")
    zeros_ready, dummies_zeroed, tiles_zeroed = sem("zeros_ready"), sem("dummies_zeroed"), sem("tiles_zeroed")
    quarter_zeroed = sem("quarter_zeroed")
    small_cleared, small_landed = sem("small_cleared"), sem("small_landed")
    dve_step, pool_step, turned_copied = sem("dve_step"), sem("pool_step"), sem("turned_copied")
    keys_ready, keys_stored = sem("keys_ready"), sem("keys_stored")
    extremes_ready, extremes_turned = sem("extremes_ready"), sem("extremes_turned")
    needs_ready, group_started = sem("needs_ready"), sem("group_started")
    row_landed = [sem(f"row_landed{b}") for b in range(2)]
    compared, equal_ready = sem("compared"), sem("equal_ready")
    totals_ready, cells_ready = sem("totals_ready"), sem("cells_ready")
    scattered, group_taken = sem("scattered"), sem("group_taken")
    turned_ready = sem("turned_ready")
    firsts_ready, totals_free = sem("firsts_ready"), sem("totals_free")
    half_landed = [sem(f"half_landed{f}") for f in range(2)]
    cells_landed, w_split, c_split = sem("cells_landed"), sem("w_split"), sem("c_split")
    var_ready, std_ready = sem("var_ready_a"), sem("std_ready_a")
    stored = [sem(f"tiles_stored{b}") for b in range(2)]

    def edge_dmas(sp, tile, dram, landed):
        sp.dma_start(tile[:, 0:FULL * G].rearrange("p (g j) -> p g j", j=G),
                     dram[0:FULL * GE].rearrange("(g p j) -> p g j", p=P, j=G)).then_inc(landed, 16)
        sp.dma_start(tile[0:REST, FULL * G:ECP],
                     dram[FULL * GE:E].rearrange("(p j) -> p j", j=G)).then_inc(landed, 16)

    with nc.Block() as block:
        @block.sync
        def _(sp):
            sp.wait_ge(edges_cleared, 3)
            edge_dmas(sp, src_i, src, edges_landed)
            edge_dmas(sp, dst_i, dst, edges_landed)
            edge_dmas(sp, w_e, edge_weight, weights_landed)
            sp.wait_ge(keys_ready, 1)
            sp.dma_start(keys_dram.rearrange("g (p j) -> p g j", j=G),
                         keys[:].rearrange("p (g j) -> p g j", j=G)).then_inc(keys_stored, 16)
            sp.wait_ge(keys_stored, 16)

            def load_row(g, b):
                sp.dma_start(key_row[:, b, :], keys_dram[bass.ds(g, 1), :].to_broadcast([P, GE])
                             ).then_inc(row_landed[b], 16)

            for b in range(2):
                load_row(b, b)
            sp.wait_ge(small_cleared, 3)
            small = [(k["x"][:, 0:T - 1, :], x[0:(T - 1) * P].rearrange("(t p) f -> p t f", p=P)),
                     (k["x"][0:LAST, T - 1, :], x[(T - 1) * P:N]),
                     (self_in[:], W_self), (neigh_in[:, 0], W_neigh), (neigh_in[:, 1], W_neigh),
                     (k["qk"][:, 0:D], qTrans), (k["qk"][:, D:2 * D], kTrans), (k["v"][:], vTrans)]
            for g, w in enumerate((Wxz, Wxh)):
                cols = slice(g * D, (g + 1) * D)
                small += [(k["cheb0"][0:D, cols], w[0]), (cheb2_in[:, cols], w[2])]
                for half in range(2):
                    rows = slice(half * D, (half + 1) * D)
                    small += [(k["cheb1"][rows, cols], w[1]), (k["cheb2"][rows, cols], w[2])]
            for to, frm in small:
                sp.dma_start(to, frm).then_inc(small_landed, 16)
            row = slice(D, D + 1)
            for to, frm in ((k["w_self"][row, :], b_self), (bias_in[row, 0:D], b_neigh),
                            (k["cheb0"][row, 0:D], bxz), (bias_in[row, D:2 * D], bhz),
                            (k["cheb0"][row, D:2 * D], bxh), (bias_in[row, 2 * D:3 * D], bhh)):
                sp.dma_start(to, frm.rearrange("(a f) -> a f", a=1)).then_inc(small_landed, 16)

            def next_row(g, b):
                sp.wait_ge(compared, g - 1)
                load_row(g, b)

            with sp.Fori(1, NG // 2) as i:
                for b in range(2):
                    next_row(2 * i + b, b)
            next_row(NG - 1, 0)

        @block.scalar
        def _(act):
            act.wait_ge(zeros_ready, 1)
            act.wait_ge(row_landed[1], 16)
            blocks = table[0:CELLS].rearrange("(t p c) two -> t p (c two)", p=P, c=NR)
            act.dma_start(table[CELLS:CELLS + GE].rearrange("(p j) two -> p (j two)", p=P),
                          zeros[:, 0:2 * G]).then_inc(dummies_zeroed, 16)

            def zero_tile(t):
                for quarter in range(4):
                    cols = slice(quarter * ZEROS, (quarter + 1) * ZEROS)
                    act.dma_start(blocks[bass.ds(t, 1), :, cols].rearrange("a p c -> (a p) c"), zeros[:]
                                  ).then_inc(quarter_zeroed, 16)
                act.wait_ge(quarter_zeroed, 64 * t + 64)
                act.sem_inc(tiles_zeroed, 1)

            for t in range(ZEROED_AHEAD):
                zero_tile(t)
            act.wait_ge(needs_ready, 4)
            with act.Fori(ZEROED_AHEAD, T) as t:
                start = act.value_load(zero_need[0:1, bass.ds(t, 1)], min_val=1, max_val=T)
                act.wait_ge(group_started, start)
                zero_tile(t)
            whole = table[0:CELLS].rearrange("(d s p c) two -> d p s (c two)", d=T, p=P, c=P)
            for b in range(2):
                act.sem_inc(stored[b], 32)

            def load(t):
                need = act.value_load(load_need[0:1, bass.ds(t, 1)], min_val=LANDED, max_val=LANDED * NG)
                act.wait_ge(scattered, need)
                act.dma_start(cells[:].rearrange("p s c two -> p s (c two)"),
                              whole[bass.ds(t, 1)].rearrange("a p s c -> (a p) s c")).then_inc(cells_landed, 16)

            def split(t, b, n):
                act.wait_ge(cells_landed, 16 * t + 16)
                act.wait_ge(stored[b], 32 * n + 32)
                for s in range(T):
                    ins = nc.scalar.activation(w_tile[:, b, s], cells[:, s, :, 0], ACT.Copy,
                                               accum_out=deg_parts[:, s, bass.ds(t, 1)])
                ins.then_inc(w_split, 1)
                nc.scalar.copy(c_tile[:, b], cells[:, :, :, 1]).then_inc(c_split, 1)

            def store(t, b):
                start = act.value_load(store_need[0:1, bass.ds(t, 1)], min_val=LANDED, max_val=LANDED * NG)
                act.wait_ge(scattered, start)
                for matrix, tile in ((weights_dram, w_tile), (counts_dram, c_tile)):
                    act.dma_start(matrix.rearrange("(s p) d -> p s d", p=P)[:, :, bass.ds(t * P, P)], tile[:, b]
                                  ).then_inc(stored[b], 16)

            def split_done(t):
                act.wait_ge(w_split, t + 1)
                act.wait_ge(c_split, t + 1)

            load(0)
            split(0, 0, 0)
            with act.Fori(0, PAIRS - 1) as i:
                for b in range(2):
                    t = 2 * i + b
                    split_done(t)
                    load(t + 1)
                    store(t, b)
                    split(t + 1, 1 - b, i + b)
            split_done(T - 3)
            load(T - 2)
            store(T - 3, 0)
            split(T - 2, 1, PAIRS - 1)
            split_done(T - 2)
            act.wait_ge(scattered, LANDED * NG)
            halves = (slice(0, PAIRS), slice(PAIRS, T))
            for f, half in enumerate(halves):
                act.dma_start(cells[:, half].rearrange("p s c two -> p s (c two)"),
                              whole[T - 1, :, half]).then_inc(half_landed[f], 16)
            store(T - 2, 1)
            act.wait_ge(stored[0], 32 * PAIRS + 32)
            for f, half in enumerate(halves):
                act.wait_ge(half_landed[f], 16)
                for s in range(half.start, half.stop):
                    ins = nc.scalar.activation(w_tile[:, 0, s], cells[:, s, :, 0], ACT.Copy,
                                               accum_out=deg_parts[:, s, T - 1:T])
                ins.then_inc(w_split, 1)
                nc.scalar.copy(c_tile[:, 0, half], cells[:, half, :, 1]).then_inc(c_split, 1)
                split_done(T - 1 + f)
                for matrix, tile in ((weights_dram, w_tile), (counts_dram, c_tile)):
                    act.dma_start(matrix.rearrange("(s p) d -> p s d", p=P)[:, half, (T - 1) * P:T * P], tile[:, 0, half]
                                  ).then_inc(stored[0], 16)
            act.wait_ge(turned_ready, 1)
            nc.scalar.copy(k["w_neigh"][:], turned[:, 0, 0:D]).then_inc(turned_copied, 1)
            nc.scalar.copy(k["w_self"][0:D, :], turned[0:D, 0, D:2 * D]).then_inc(turned_copied, 1)
            act.wait_ge(var_ready, 1)
            nc.scalar.activation(k["stat"][:, 2], k["stat"][:, 1], ACT.Sqrt).then_inc(std_ready, 1)
            act.wait_ge(stored[0], 32 * (PAIRS + 3))
            act.wait_ge(stored[1], 32 * (PAIRS + 1))

        @block.vector
        def _(dve):
            steps = [0]

            def link(ins):
                steps[0] += 1
                ins.then_inc(dve_step, 1)
                dve.wait_ge(dve_step, steps[0])

            nc.vector.memset(src_i[:], PAD).then_inc(edges_cleared, 1)
            nc.vector.memset(dst_i[:], PAD).then_inc(edges_cleared, 1)
            nc.vector.memset(w_e[:], 0.0).then_inc(edges_cleared, 1)
            nc.vector.memset(zeros[:], 0.0).then_inc(zeros_ready, 1)
            nc.vector.memset(k["x"][:, T - 1, :], 0.0).then_inc(small_cleared, 1)
            nc.vector.memset(ones_bf[:], 1.0).then_inc(small_cleared, 1)
            nc.vector.memset(zero_bf[:], 0.0).then_inc(small_cleared, 1)
            link(nc.vector.memset(ones_f[:], 1.0))
            link(nc.vector.memset(parts[:, :, 4:5], 1.0))
            dve.wait_ge(edges_landed, 16 * 4)
            link(nc.vector.tensor_scalar(dst_tile[:], dst_i[:], P.bit_length() - 1, None, ALU.logical_shift_right))
            link(nc.vector.scalar_tensor_tensor(keys[:], src_i[:], float(P), dst_i[:], ALU.mult, ALU.add))
            nc.vector.scalar_tensor_tensor(keys[:], dst_tile[:], float(TILE_CELLS - P), keys[:], ALU.mult, ALU.add
                                           ).then_inc(keys_ready, 1)
            dve.wait_ge(keys_ready, 1)
            link(nc.vector.tensor_scalar(dst_i[:], dst_i[:], P - 1, None, ALU.bitwise_and))
            of_groups = dst_tile[:].rearrange("p (g j) -> p g j", j=G)
            nc.vector.tensor_reduce(extremes[:, 0], of_groups, AX.X, ALU.max)
            nc.vector.tensor_reduce(extremes[:, 1], of_groups, AX.X, ALU.min).then_inc(extremes_ready, 1)
            dve.wait_ge(weights_landed, 16 * 2)
            link(nc.vector.tensor_copy(parts[:, :, 0], w_e[:]))
            link(nc.vector.tensor_tensor(w_e[:], w_e[:], parts[:, :, 0], ALU.subtract))
            link(nc.vector.tensor_copy(parts[:, :, 1], w_e[:]))
            link(nc.vector.tensor_tensor(w_e[:], w_e[:], parts[:, :, 1], ALU.subtract))
            link(nc.vector.tensor_copy(parts[:, :, 2], w_e[:]))
            dve.wait_ge(pool_step, 2)
            link(nc.vector.memset(parts[:, 0:FULL * G, 3:4], 1.0))
            link(nc.vector.tensor_scalar(parts[:, FULL * G:ECP, 3], partition[:], float(REST), None, ALU.is_lt))
            dve.wait_ge(extremes_turned, 1)
            nc.vector.tensor_reduce(group_extremes[:, 0:1], turned[0:NG, 1, 0:P], AX.X, ALU.max)
            link(nc.vector.tensor_reduce(group_extremes[:, 1:2], turned[0:NG, 1, P:2 * P], AX.X, ALU.min))
            dve.wait_ge(pool_step, 8)
            nc.vector.tensor_scalar(uses[:, 1], tiles_iota[0:NG, :], group_extremes[:, 0:1], group_less[0:NG, :],
                                    ALU.is_le, ALU.mult)
            nc.vector.tensor_scalar(uses[:, 0], tiles_iota[0:NG, :], group_extremes[:, 1:2], landed_count[0:NG, :],
                                    ALU.is_ge, ALU.mult).then_inc(extremes_ready, 1)
            dve.wait_ge(extremes_turned, 2)
            nc.vector.tensor_scalar(zeroed_need[:], turned[0:1, 1, 0:NG], 1.0, None, ALU.add).then_inc(needs_ready, 1)
            nc.vector.tensor_reduce(tile_uses[:, 0:1], turned[0:T, 1, P:P + NG], AX.X, ALU.max)
            nc.vector.tensor_reduce(tile_uses[:, 1:2], turned[0:T, 1, 2 * P:2 * P + NG], AX.X, ALU.min
                                    ).then_inc(extremes_ready, 1)
            link(nc.vector.tensor_scalar(schedule[:, 0], tiles_iota[0:1, :], float(LOAD_EVERY * LANDED),
                                         float(LOADS_FROM * LANDED), ALU.mult, ALU.add))
            link(nc.vector.tensor_scalar(schedule[:, 1], tiles_iota[0:1, :], float(1 - ZEROED_AHEAD), None, ALU.add))
            link(nc.vector.memset(load_at[:, T:T + 1], float(NG * LANDED)))
            dve.wait_ge(extremes_turned, 3)
            link(nc.vector.tensor_tensor(load_at[:, 0:T], turned[0:1, 1, 0:T], schedule[:, 0], ALU.max))
            nc.vector.tensor_copy(load_need[:], load_at[:, 0:T]).then_inc(needs_ready, 1)
            nc.vector.tensor_scalar(store_need[:], load_at[:, 1:T + 1], float(LANDED), float(NG * LANDED),
                                    ALU.add, ALU.min).then_inc(needs_ready, 1)
            nc.vector.scalar_tensor_tensor(zero_need[:], turned[0:1, 1, P:P + T], float(NG + 1), schedule[:, 1],
                                           ALU.add, ALU.min).then_inc(needs_ready, 1)

            def compare(g, b, columns):
                for j in columns:
                    ins = nc.vector.tensor_scalar(equal[b][:, j * GE:(j + 1) * GE], key_row[:, b, :],
                                                  keys[:, bass.ds(g * G + j, 1)], None, ALU.is_equal)
                return ins

            def compare_rest(g, b, first):
                compare(g, b, range(first, G)).then_inc(compared, 1)
                edges = bass.ds(g * G, G)
                nc.vector.tensor_copy(parts_g[:, b], parts[:, edges, :])
                nc.vector.tensor_tensor(keys_rel[:, b], keys[:, edges], dummy[:], ALU.subtract)
                nc.vector.tensor_tensor(is_row[:, b], rows_iota[:].unsqueeze(1).to_broadcast([P, G, P]),
                                        dst_i[:, edges].unsqueeze(2).to_broadcast([P, G, P]), ALU.is_equal)
                nc.vector.tensor_tensor(is_tile[:, b], tiles_iota[:].unsqueeze(1).to_broadcast([P, G, T]),
                                        dst_tile[:, edges].unsqueeze(2).to_broadcast([P, G, T]), ALU.is_equal)
                dve.wait_ge(compared, g + 1)
                diagonal = equal[b][:].rearrange("p (j r) -> p j r", j=G)[:, :, 0:GE:G]
                nc.vector.tensor_tensor(equal_earlier[:, b], diagonal,
                                        earlier[:].unsqueeze(1).to_broadcast([P, G, P]), ALU.mult
                                        ).then_inc(equal_ready, 1)

            def choose_cells(g, b):
                dve.wait_ge(totals_ready, g + 1)
                sums = totals[:, b, 0:8 * G].rearrange("p (j c) -> p j c", c=8)
                nc.vector.scalar_tensor_tensor(first_rel[:, b], sums[:, :, 4], 0.0, keys_rel[:, b],
                                               ALU.is_equal, ALU.mult).then_inc(firsts_ready, 1)
                dve.wait_ge(firsts_ready, g + 1)
                nc.vector.tensor_reduce(amount[:, b, :, 0], sums[:, :, 0:3], AX.X, ALU.add)
                nc.vector.tensor_copy(amount[:, b, :, 1], sums[:, :, 3]).then_inc(totals_free, 1)
                nc.vector.tensor_tensor(cell[:, b], first_rel[:, b], dummy[:], ALU.add).then_inc(cells_ready, 1)

            dve.sem_inc(totals_free, 2)
            EARLY = 4

            def next_group(g, b, n):
                dve.wait_ge(row_landed[b], 16 * n + 16)
                compare(g, b, range(EARLY))
                dve.wait_ge(group_taken, g)
                choose_cells(g - 1, 1 - b)
                compare_rest(g, b, EARLY)

            dve.wait_ge(row_landed[0], 16)
            compare_rest(0, 0, 0)
            with dve.Fori(0, NG // 2) as i:
                next_group(2 * i + 1, 1, i)
                next_group(2 * i + 2, 0, i + 1)
            dve.wait_ge(group_taken, NG)
            choose_cells(NG - 1, 0)
            dve.wait_ge(small_landed, 16 * SMALL)
            row = slice(D, D + 1)
            link(nc.vector.tensor_tensor(k["cheb0"][0:D, :], k["cheb0"][0:D, :], cheb2_in[:], ALU.subtract))
            link(nc.vector.tensor_scalar(k["cheb2"][:], k["cheb2"][:], 2.0, None, ALU.mult))
            link(nc.vector.tensor_tensor(k["w_self"][row, :], k["w_self"][row, :], bias_in[row, 0:D], ALU.add))
            link(nc.vector.tensor_tensor(k["cheb0"][row, :], k["cheb0"][row, :], bias_in[row, D:3 * D], ALU.add))
            link(nc.vector.tensor_copy(k["deg_in"][:], degrees[:, 0:T]))
            layer_norm(nc, dve, link, k["x"], k["h"], centred, k["stat"], var_ready, std_ready, 0)
            dve.wait_ge(w_split, T + 1)
            link(nc.vector.tensor_reduce(k["deg_out"][:], deg_parts[:], AX.X, ALU.add))

        @block.tensor
        def _(pe):
            pe.wait_ge(pool_step, 4)
            pe.wait_ge(extremes_ready, 1)
            nc.tensor.transpose(turned[0:NG, 1, 0:P], extremes[:, 0], k["ident"][:])
            nc.tensor.transpose(turned[0:NG, 1, P:2 * P], extremes[:, 1], k["ident"][:]).then_inc(extremes_turned, 1)
            pe.wait_ge(extremes_ready, 2)
            nc.tensor.matmul(turned[0:1, 1, 0:NG], group_extremes[:, 0:1], k["ident"][0:NG, 0:NG], start=True, stop=True)
            for n in range(2):
                ins = nc.tensor.transpose(turned[0:T, 1, (n + 1) * P:(n + 1) * P + NG], uses[:, n],
                                          k["ident"][0:NG, 0:NG])
            ins.then_inc(extremes_turned, 1)
            pe.wait_ge(extremes_ready, 3)
            pe.wait_ge(needs_ready, 1)
            for n in range(2):
                ins = nc.tensor.matmul(turned[0:1, 1, n * P:n * P + T], tile_uses[:, n:n + 1], k["ident"][0:T, 0:T],
                                       start=True, stop=True, skip_group_check=True)
            ins.then_inc(extremes_turned, 1)
            nc.tensor.matmul(degrees[:, 0:T], zero_bf[:], zero_bf[:, 0:T], start=True, stop=False, skip_group_check=True)

            def add_up(g, b):
                pe.wait_ge(totals_free, g + 1)
                pe.wait_ge(equal_ready, g + 1)
                by_column = equal[b][:, 0:G * GE].rearrange("p (j q m) -> p j m q", j=G, m=G)
                for m in range(G):
                    sums = totals[:, b, 8 * m:8 * m + 5]
                    for j in range(G):
                        cols = 5 if j < m else 4
                        nc.tensor.matmul(sums[:, 0:cols], by_column[:, j, m, :], parts_g[:, b, j, 0:cols],
                                         start=(j == 0), stop=(j == G - 1), skip_group_check=True)
                    nc.tensor.matmul(sums[:, 4:5], equal_earlier[:, b, m, :], ones_bf[:, 0:1],
                                     start=(m == 0), stop=True, skip_group_check=True)
                for j in range(G):
                    ins = nc.tensor.matmul(degrees[:, 0:T], is_row[:, b, j, :], is_tile[:, b, j, :], start=False,
                                           stop=True, skip_group_check=True)
                ins.then_inc(totals_ready, 1)

            with pe.Fori(0, NG // 2) as i:
                for b in range(2):
                    add_up(2 * i + b, b)
            add_up(NG - 1, 0)
            pe.wait_ge(small_landed, 16 * SMALL)
            nc.tensor.transpose(turned[:, 0, 0:D], neigh_in[:].rearrange("p a f -> p (a f)"), k["ident"][0:D, 0:D])
            nc.tensor.transpose(turned[0:D, 0, D:2 * D], self_in[:], k["ident"][0:D, 0:D]).then_inc(turned_ready, 1)

        @block.gpsimd
        def _(pool):
            nc.gpsimd.iota(dummy[:], pattern=[[P, G]], base=CELLS, channel_multiplier=1,
                           allow_small_or_imprecise_dtypes=True).then_inc(pool_step, 1)
            nc.gpsimd.iota(partition[:], pattern=[[0, G]], base=0, channel_multiplier=1,
                           allow_small_or_imprecise_dtypes=True).then_inc(pool_step, 1)
            pool.wait_ge(small_cleared, 3)
            nc.gpsimd.affine_select(out=earlier[:], in_=ones_bf[:], compare_op=ALU.is_gt, fill=0.0, base=0,
                                    pattern=[[1, P]], channel_multiplier=-1).then_inc(pool_step, 1)
            pool.wait_ge(dve_step, 1)
            nc.gpsimd.affine_select(out=k["ident"][:], in_=ones_f[:], compare_op=ALU.is_equal, fill=0.0, base=0,
                                    pattern=[[-1, P]], channel_multiplier=1).then_inc(pool_step, 1)
            nc.gpsimd.iota(rows_iota[:], pattern=[[1, P]], base=0, channel_multiplier=0,
                           allow_small_or_imprecise_dtypes=True).then_inc(pool_step, 1)
            nc.gpsimd.iota(tiles_iota[:], pattern=[[1, T]], base=0, channel_multiplier=0,
                           allow_small_or_imprecise_dtypes=True).then_inc(pool_step, 1)
            nc.gpsimd.iota(landed_count[:], pattern=[[1, 1]], base=LANDED, channel_multiplier=LANDED,
                           allow_small_or_imprecise_dtypes=True).then_inc(pool_step, 1)
            nc.gpsimd.iota(group_less[:], pattern=[[1, 1]], base=-NG, channel_multiplier=1,
                           allow_small_or_imprecise_dtypes=True).then_inc(pool_step, 1)
            pool.wait_ge(needs_ready, 4)
            pool.wait_ge(dummies_zeroed, 16)

            def scatter(g, b):
                pool.sem_inc(group_started, 1)
                need = pool.value_load(zeroed_need[0:1, bass.ds(g, 1)], min_val=1, max_val=T)
                pool.wait_ge(tiles_zeroed, need)
                pool.sem_inc(group_taken, 1)
                for j in range(G):
                    nc.gpsimd.indirect_dma_start(
                        out=table, out_offset=bass.IndirectOffsetOnAxis(ap=cell[:, b, j:j + 1], axis=0),
                        in_=amount[:, b, j, :], in_offset=None, compute_op=ALU.add).then_inc(scattered, 16)

            pool.sem_inc(group_taken, 1)
            pool.wait_ge(cells_ready, 1)
            scatter(0, 0)
            pool.wait_ge(cells_ready, 2)
            pool.wait_ge(scattered, LANDED)
            scatter(1, 1)
            with pool.Fori(1, NG // 2) as i:
                for b in range(2):
                    pool.wait_ge(cells_ready, 2 * i + b + 1)
                    pool.wait_ge(scattered, (2 * i + b) * LANDED)
                    scatter(2 * i + b, b)
            pool.wait_ge(cells_ready, NG)
            pool.wait_ge(scattered, (NG - 1) * LANDED)
            scatter(NG - 1, 0)
            pool.wait_ge(scattered, LANDED * NG)


def layer_norm(nc, dve, link, x, h, centred, stat, var_ready, std_ready, layer):
    whole = [P, T, D]
    link(nc.vector.tensor_reduce(stat[:, 0], x[:], AX.X, ALU.add))
    link(nc.vector.scalar_tensor_tensor(centred[:], stat[:, 0].unsqueeze(2).to_broadcast(whole), -1.0 / D, x[:],
                                        ALU.mult, ALU.add))
    link(nc.vector.tensor_tensor(h[:], centred[:], centred[:], ALU.mult))
    link(nc.vector.tensor_reduce(stat[:, 1], h[:], AX.X, ALU.add))
    nc.vector.tensor_scalar(stat[:, 1], stat[:, 1], 1.0 / D, EPS, ALU.mult, ALU.add).then_inc(var_ready, 1)
    dve.wait_ge(std_ready, layer + 1)
    link(nc.vector.reciprocal(stat[:, 0], stat[:, 2]))
    link(nc.vector.scalar_tensor_tensor(h[:], centred[:], 0.0, stat[:, 0].unsqueeze(2).to_broadcast(whole),
                                        ALU.max, ALU.mult))


def propagating_layers(nc, c, k, sb, weights_dram, counts_dram):
    def sem(name):
        return c.enter_context(nc.semaphore(name))

    x = k["x"]
    h, stat = k["h"], k["stat"]
    xs, tmp = sb("xs", [P, T, D], F32, c), sb("tmp", [P, T, D], F32, c)
    gate = sb("gate", [P, T, 2 * D], F32, c)
    acc = gate[:].rearrange("p t f -> p (t f)")[:, 0:T * D].rearrange("p (t f) -> p t f", f=D)
    h_t = sb("h_t", [D + 1, NR], F32, c)
    y_t = sb("y_t", [P, NR], F32, c)
    tiles = sb("tiles", [P, 2, 2, NR], F32, c)
    resident = sb("resident", [P, KEPT, NR], F32, c)
    gate_2 = resident[:, 1].rearrange("p (t f) -> p t f", f=2 * D)
    y2_t = resident[:, 0]
    xs_pair = sb("xs_pair", [P, 2, 2, D], F32, c)
    clipped, scale = sb("deg_clipped", [P, 2, T], F32, c), sb("scale", [P, 6, T], F32, c)
    DINV, DIS, NDIS, INV, ROOT, TWICE = range(6)
    zero_row = sb("zero_row_c", [1, BANK], BF16, c)
    banks = c.enter_context(nc.psum_tensor("banks", [P, 8, BANK], F32))
    flat = banks[:].rearrange("p a b -> p (a b)")

    stages = ["sums0", "nodes0", "sums1", "nodes1", "sums2", "nodes2", "sums3", "linear3", "sums4", "nodes4",
              "sums5", "gate_neigh"]
    order = {name: n for n, name in enumerate(stages)}

    def order_of_sums(prop):
        return 2 * prop

    banks_filled, banks_read = sem("banks_filled"), sem("banks_read")
    tmp_free, even_copied = sem("tmp_free"), sem("even_copied")
    banks_copied = sem("banks_copied")
    side_filled, side_read = sem("side_filled"), sem("side_read")
    consts_set, dve_step = sem("consts_set"), sem("dve_step_c")
    var_ready, std_ready = sem("var_ready"), sem("std_ready")
    deg_ready, root_ready = sem("deg_clipped_ready"), sem("deg_root_ready")
    xs_ready = sem("xs_ready")
    half_filled, gate_ready, gate_done = sem("half_filled"), sem("gate_ready"), sem("gate_done")
    gate_halves = (slice(0, 4 * BANK // P), slice(4 * BANK // P, T))
    tiles_landed = [[sem(f"tiles_landed{b}{f}") for f in range(2)] for b in range(2)]
    slot_free = [[sem(f"slot_free{b}{f}") for f in range(2)] for b in range(2)]
    ENDS = (0, 3, len(CHUNKS))
    pair_ready = [sem(f"pair_ready{b}") for b in range(2)]
    resident_landed, resident_used = sem("resident_landed"), sem("resident_used")
    USES = (STREAMED // 4 + 1, STREAMED // 4)

    with nc.Block() as block:
        @block.sync
        def _(sp):
            def load(dram, prop, first):
                matrix = dram.rearrange("(t p) d -> p t d", p=P)

                def stream(i, slots=(0, 1)):
                    for b in slots:
                        for f in range(2):
                            cols = slice(CHUNKS[ENDS[f]][0], sum(CHUNKS[ENDS[f + 1] - 1]))
                            sp.wait_ge(slot_free[b][f], USES[b] * prop + i + 1)
                            sp.dma_start(tiles[:, b, :, cols], matrix[:, bass.ds(4 * i + 2 * b, 2), cols]
                                         ).then_inc(tiles_landed[b][f], 16)

                stream(0)
                if first:
                    if prop:
                        sp.wait_ge(resident_used, prop)
                    sp.dma_start(resident[:], matrix[:, STREAMED:T, :]).then_inc(resident_landed, 16)
                with sp.Fori(1, USES[1]) as i:
                    stream(i)
                stream(USES[1], (0,))

            for dram, prop in ((counts_dram, 0), (weights_dram, 3)):
                load(dram, prop, True)
                with sp.Fori(prop + 1, prop + 3) as other:
                    load(dram, other, False)

        @block.scalar
        def _(act):
            def root(layer):
                act.wait_ge(var_ready, layer + 1)
                nc.scalar.activation(stat[:, 2], stat[:, 1], ACT.Sqrt).then_inc(std_ready, 1)

            def copy_sums(prop, to):
                act.wait_ge(banks_filled, order_of_sums(prop) + 1)
                for n, (c0, w) in enumerate(CHUNKS):
                    nc.scalar.copy(to[:, c0:c0 + w], banks[:, n, 0:w]).then_inc(banks_copied, 1)
                act.wait_ge(banks_copied, len(CHUNKS) * (prop + 1))
                act.sem_inc(banks_read, 1)

            def copy_even(prop, n):
                act.wait_ge(banks_filled, order_of_sums(prop) + 2)
                act.wait_ge(tmp_free, n + 1)
                nc.scalar.copy(tmp[:], flat[:, 0:T * P].rearrange("p (t a f) -> p t a f", a=2, f=D)[:, :, 0]
                               ).then_inc(even_copied, 1)

            def feed(prop, to=y_t):
                act.wait_ge(xs_ready, prop + 1)
                def stage(i, b):
                    act.wait_ge(slot_free[b][1], USES[b] * prop + i + 1)
                    nc.scalar.copy(xs_pair[:, b], xs[:, bass.ds(4 * i + 2 * b, 2), :]).then_inc(pair_ready[b], 1)

                with act.Fori(0, USES[1]) as i:
                    for b in range(2):
                        stage(i, b)
                stage(USES[1], 0)
                copy_sums(prop, to)

            act.wait_ge(deg_ready, 1)
            nc.scalar.activation(scale[:, DINV:DIS + 1], clipped[:], ACT.Sqrt).then_inc(root_ready, 1)
            with act.Fori(0, 3) as prop:
                feed(prop)
                copy_even(prop, prop)
            root(0)
            feed(3)
            root(1)
            feed(4)
            copy_even(4, 4)
            feed(5, y2_t)
            for f, ts in enumerate(gate_halves):
                act.wait_ge(gate_ready, f + 1)
                nc.scalar.activation(tmp[:, ts], gate[:, ts, 0:D], ACT.Sigmoid, scale=-1.0).then_inc(gate_done, 1)
                nc.scalar.activation(h[:, ts], gate[:, ts, D:2 * D], ACT.Tanh).then_inc(gate_done, 1)

        @block.vector
        def _(dve):
            steps = [0]

            def link(ins):
                steps[0] += 1
                ins.then_inc(dve_step, 1)
                dve.wait_ge(dve_step, steps[0])

            def add_halves(stage):
                halves = flat[:, 0:T * P].rearrange("p (t a f) -> p t a f", a=2, f=D)
                evens[0] += 1
                dve.wait_ge(even_copied, evens[0])
                nc.vector.tensor_tensor(tmp[:], tmp[:], halves[:, :, 1], ALU.add).then_inc(banks_read, 1)
                dve.wait_ge(banks_read, order[stage] + 2)

            def per_node(n, width=D):
                return scale[:, n].unsqueeze(2).to_broadcast([P, T, width])

            sides, evens = [0], [0]

            def side(width, rows=slice(0, P)):
                for c0, w in CHUNKS:
                    sides[0] += 1
                    dve.wait_ge(side_filled, sides[0])
                    yield c0 // P, w // P, banks[rows, 7, 0:w // P * width]

            def done(ins):
                ins.then_inc(side_read, 1)

            def turned():
                for t, n, cols in side(P, slice(0, D)):
                    done(nc.vector.tensor_copy(h_t[0:D, t * P:(t + n) * P], cols))

            dve.sem_inc(tmp_free, 1)
            nc.vector.memset(zero_row[:], 0.0).then_inc(consts_set, 1)
            link(nc.vector.tensor_scalar(scale[:, ROOT], k["deg_out"][:], 0.0, None, ALU.is_gt))
            link(nc.vector.tensor_tensor(clipped[:, 1], k["deg_out"][:], scale[:, ROOT], ALU.mult))
            link(nc.vector.tensor_scalar(scale[:, INV], scale[:, ROOT], -1.0, 1.0, ALU.mult, ALU.add))
            link(nc.vector.tensor_tensor(clipped[:, 1], clipped[:, 1], scale[:, INV], ALU.max))
            nc.vector.tensor_scalar(clipped[:, 0], k["deg_in"][:], 1.0, None, ALU.max).then_inc(deg_ready, 1)
            dve.wait_ge(deg_ready, 1)
            link(nc.vector.reciprocal(scale[:, INV], clipped[:, 0]))
            dve.wait_ge(root_ready, 1)
            link(nc.vector.reciprocal(scale[:, DINV:DIS + 1], scale[:, DINV:DIS + 1]))
            link(nc.vector.tensor_tensor(scale[:, DIS], scale[:, DIS], scale[:, ROOT], ALU.mult))
            link(nc.vector.tensor_scalar(scale[:, NDIS], scale[:, DIS], -1.0, None, ALU.mult))
            link(nc.vector.tensor_scalar(scale[:, ROOT], k["deg_in"][:], 0.0, None, ALU.is_gt))
            link(nc.vector.tensor_tensor(scale[:, DINV], scale[:, DINV], scale[:, ROOT], ALU.mult))
            link(nc.vector.tensor_tensor(scale[:, TWICE], scale[:, DINV], scale[:, DINV], ALU.mult))

            nc.vector.tensor_tensor(xs[:], h[:], per_node(DINV), ALU.mult).then_inc(xs_ready, 1)
            link(nc.vector.memset(h_t[D:D + 1, :], 1.0))
            for prop in range(3):
                add_halves(f"nodes{prop}")
                if prop < 2:
                    nc.vector.tensor_tensor(xs[:], tmp[:], per_node(TWICE), ALU.mult).then_inc(xs_ready, 1)
                    dve.wait_ge(xs_ready, prop + 2)
                link(nc.vector.tensor_tensor(tmp[:], tmp[:], per_node(DINV), ALU.mult))
                link(nc.vector.tensor_tensor(acc[:], acc[:] if prop else h[:], tmp[:], ALU.add))
                dve.sem_inc(tmp_free, 1)
            link(nc.vector.scalar_tensor_tensor(x[:], acc[:], 0.25, x[:], ALU.mult, ALU.add))

            layer_norm(nc, dve, link, x, h, tmp, stat, var_ready, std_ready, 0)
            nc.vector.tensor_copy(xs[:], h[:]).then_inc(xs_ready, 1)
            turned()
            for t, n, cols in side(D):
                done(nc.vector.tensor_tensor(x[:, t:t + n], cols.rearrange("p (t f) -> p t f", f=D), x[:, t:t + n],
                                             ALU.add))
            dve.wait_ge(banks_filled, order["linear3"] + 1)
            near = flat[:, 0:T * D].rearrange("p (t f) -> p t f", f=D)
            nc.vector.tensor_tensor(tmp[:], near, per_node(INV), ALU.mult).then_inc(banks_read, 1)
            dve.wait_ge(banks_read, order["linear3"] + 2)
            dve.wait_ge(side_read, sides[0] + 1)
            link(nc.vector.tensor_tensor(x[:], x[:], tmp[:], ALU.add))

            layer_norm(nc, dve, link, x, h, tmp, stat, var_ready, std_ready, 1)
            nc.vector.tensor_tensor(xs[:], h[:], per_node(DIS), ALU.mult).then_inc(xs_ready, 1)
            link(nc.vector.tensor_tensor(scale[:, TWICE], scale[:, DIS], scale[:, NDIS], ALU.mult))
            turned()
            for t, n, cols in side(2 * D):
                done(nc.vector.tensor_copy(gate[:, t:t + n], cols.rearrange("p (t f) -> p t f", f=2 * D)))
            dve.sem_inc(tmp_free, 1)
            add_halves("nodes4")
            nc.vector.tensor_tensor(xs[:], tmp[:], per_node(TWICE), ALU.mult).then_inc(xs_ready, 1)
            dve.wait_ge(xs_ready, 6)
            for t, n, cols in side(2 * D):
                four = tmp[:].rearrange("p t f -> p (t f)")[:, 0:n * 2 * D].rearrange("p (t f) -> p t f", f=2 * D)
                done(nc.vector.tensor_tensor(four, cols.rearrange("p (t f) -> p t f", f=2 * D),
                                             scale[:, NDIS, t:t + n].unsqueeze(2).to_broadcast([P, n, 2 * D]), ALU.mult))
                dve.wait_ge(side_read, sides[0] + 1)
                link(nc.vector.tensor_tensor(gate[:, t:t + n], gate[:, t:t + n], four, ALU.add))
            near = flat[:, 0:T * 2 * D].rearrange("p (t f) -> p t f", f=2 * D)
            for f, ts in enumerate(gate_halves):
                if f == 0:
                    dve.wait_ge(half_filled, 1)
                else:
                    dve.wait_ge(banks_filled, order["gate_neigh"] + 1)
                n = ts.stop - ts.start
                link(nc.vector.tensor_tensor(gate_2[:, ts], near[:, ts],
                                             scale[:, NDIS, ts].unsqueeze(2).to_broadcast([P, n, 2 * D]), ALU.mult))
                nc.vector.tensor_tensor(gate[:, ts], gate[:, ts], gate_2[:, ts], ALU.add).then_inc(gate_ready, 1)
            for f, ts in enumerate(gate_halves):
                dve.wait_ge(gate_done, 2 * f + 2)
                link(nc.vector.tensor_tensor(xs[:, ts], tmp[:, ts], h[:, ts], ALU.mult))
                link(nc.vector.tensor_tensor(x[:, ts], x[:, ts], xs[:, ts], ALU.add))

        @block.tensor
        def _(pe):
            sides = [0]

            def beside(terms, width, rows=slice(0, P)):
                def maker(c0, w):
                    def make():
                        sides[0] += 1
                        pe.wait_ge(side_read, sides[0])
                        for t in range(c0 // P, (c0 + w) // P):
                            to = banks[rows, 7, (t - c0 // P) * width:(t - c0 // P + 1) * width]
                            ins = terms(to, t)
                        ins.then_inc(side_filled, 1)
                    return make
                return [maker(c0, w) for c0, w in CHUNKS]

            def turn_h(to, t):
                return nc.tensor.transpose(to, h[:, t, :], k["ident"][:])

            def times(lhs, rhs):
                return lambda to, t: nc.tensor.matmul(to, lhs[:, t * P:(t + 1) * P], rhs, start=True, stop=True,
                                                      skip_group_check=True)

            def product(prop, matrices, side=()):
                pe.wait_ge(banks_read, order_of_sums(prop) + 1)
                for n, (c0, w) in enumerate(CHUNKS):
                    nc.tensor.matmul(banks[:, n, 0:w], zero_row[:, 0:P], zero_row[:, 0:w], start=True, stop=False,
                                     skip_group_check=True)

                def add(half, n, c0, w, features, tile):
                    return nc.tensor.matmul(banks[half * D:half * D + D, n, 0:w], features, tile[:, c0:c0 + w],
                                            start=False, stop=True, skip_group_check=True)

                points = [0]

                def streamed(i, slots=(0, 1)):
                    for b in slots:
                        pe.wait_ge(pair_ready[b], USES[b] * prop + i + 1)
                        for f in range(2):
                            for make in side[points[0] * len(side) // 16:(points[0] + 1) * len(side) // 16]:
                                make()
                            points[0] += 1
                            pe.wait_ge(tiles_landed[b][f], 16 * USES[b] * prop + 16 * i + 16)
                            for n in range(ENDS[f], ENDS[f + 1]):
                                for half in range(2):
                                    ins = add(half, n, *CHUNKS[n], xs_pair[:, b, half], tiles[:, b, half])
                            ins.then_inc(slot_free[b][f], 1)

                for i in range(USES[1]):
                    streamed(i)
                    if i == 0:
                        pe.wait_ge(resident_landed, 16 * matrices)
                    pair = range(2 * i, min(2 * i + 2, KEPT))
                    for n, (c0, w) in enumerate(CHUNKS):
                        for t in pair:
                            ins = add(t % 2, n, c0, w, xs[:, STREAMED + t], resident[:, t])
                ins.then_inc(resident_used, 1)
                streamed(USES[1], (0,))
                pe.wait_ge(slot_free[0][1], USES[0] * prop + USES[0] + 1)
                pe.wait_ge(resident_used, prop + 1)
                pe.sem_inc(banks_filled, 1)

            def by_nodes(prop, lhs, rhs, width):
                for n, (c0, w) in enumerate(CHUNKS):
                    pe.wait_ge(banks_copied, len(CHUNKS) * prop + n + 1)
                    for t in range(c0 // P, (c0 + w) // P):
                        ins = nc.tensor.matmul(flat[:, t * width:(t + 1) * width], lhs[:, t * P:(t + 1) * P], rhs,
                                               start=True, stop=True, skip_group_check=True)
                    if prop == 5 and n == 3:
                        ins.then_inc(half_filled, 1)
                ins.then_inc(banks_filled, 1)

            def turn_sums(prop):
                for n, (c0, w) in enumerate(CHUNKS):
                    pe.wait_ge(banks_copied, len(CHUNKS) * prop + n + 1)
                    for t in range(c0 // P, (c0 + w) // P):
                        ins = nc.tensor.transpose(flat[:, t * P:(t + 1) * P], y_t[:, t * P:(t + 1) * P], k["ident"][:])
                ins.then_inc(banks_filled, 1)

            for b in range(2):
                for f in range(2):
                    pe.sem_inc(slot_free[b][f], 1)
            pe.sem_inc(side_read, 1)
            pe.sem_inc(banks_read, 1)
            pe.wait_ge(consts_set, 1)
            with pe.Fori(0, 3) as prop:
                product(prop, 1)
                turn_sums(prop)
            pe.wait_ge(xs_ready, 4)
            product(3, 2, beside(turn_h, P, slice(0, D)) + beside(times(h_t, k["w_self"][:]), D))
            by_nodes(3, y_t, k["w_neigh"][:], D)
            pe.wait_ge(xs_ready, 5)
            product(4, 2, beside(turn_h, P, slice(0, D)) + beside(times(h_t, k["cheb0"][:]), 2 * D))
            turn_sums(4)
            product(5, 2, beside(times(y_t, k["cheb1"][:]), 2 * D))
            by_nodes(5, y2_t, k["cheb2"][:], 2 * D)


def attention_layer(nc, c, k, sb, counts_dram, out):
    def sem(name):
        return c.enter_context(nc.semaphore(name))

    parts_dram = nc.dram_tensor("parts_dram", [3, 2, HEADS, HD, NR], BF16, kind="Internal").ap()
    x = k["x"]
    h, stat, tmp = k["h"], k["stat"], sb("tmp_d", [P, T, D], F32, c)
    h_t = sb("h_t_d", [D, NR], F32, c)
    qk_t = sb("qk_t", [P, NR], F32, c)
    part = sb("qk_part", [P, 3, NR], BF16, c)
    q6, k6 = sb("q6", [NPART * HD, HEADS, NR], BF16, c), sb("k6", [NPART * HD, HEADS, NR], BF16, c)
    v_all = sb("v_all", [P, T, HEADS, VW], F32, c)
    v_tile = sb("v_tile", [P, RING, HEADS * VW], F32, c)
    count = sb("count", [P, RING, 4, P], F32, c)
    att = sb("att", [P, RING, HEADS, BANK], F32, c)
    shift = sb("shift", [P, 2], F32, c)
    o_t = sb("o_t", [P, NR], F32, c)
    den = sb("den", [P, T, HEADS], F32, c)
    zero_row = sb("zero_row_d", [1, BANK], BF16, c)
    banks = c.enter_context(nc.psum_tensor("banks_d", [P, 8, BANK], F32))
    flat = banks[:].rearrange("p a b -> p (a b)")
    scores, acc, count_t = banks[:, 0:4], banks[:, 4], [banks[:, n] for n in (5, 6, 7)]
    LO, HI = 4.5399929762484854e-05, 22026.465794806718

    dve_step, consts_set = sem("dve_step_d"), sem("consts_set_d")
    var_ready, std_ready = sem("var_ready_d"), sem("std_ready_d")
    h_ready, turned = sem("h_ready_d"), sem("turned_d")
    h_t_ready, qk_copied = [sem(f"h_t_ready{e}") for e in range(2)], [sem(f"qk_copied{e}") for e in range(2)]
    qk_ready, parts_ready, v_cleared = sem("qk_ready"), sem("qk_parts_ready"), sem("v_cleared")
    parts_stored = [sem(f"parts_stored{n}") for n in range(3)]
    rows_placed = sem("rows_placed")
    v_made, v_copied = sem("v_made"), sem("v_copied")
    count_landed = [sem(f"count_landed{j}") for j in range(RING)]
    counts_turned, weighted, values_added = sem("counts_turned"), sem("weighted"), sem("values_added")
    scored = [sem(f"scored{f}") for f in range(2)]
    scores_read = [sem(f"scores_read{f}") for f in range(2)]
    expd_high, clipped = sem("expd_high"), sem("clipped")
    value_taken = sem("value_taken")
    acc_full, acc_read = sem("acc_full"), sem("acc_read")
    nodes_ready, out_ready, out_stored = sem("nodes_ready_d"), sem("out_ready"), sem("out_stored")
    out_parts = (slice(0, 4 * (T // 8)), slice(4 * (T // 8), T))
    SC = T // 4

    USES = T // RING

    def over_tiles(eng, c_reg, body):
        with eng.Fori(0, T // RING) as i:
            for j in range(RING):
                body(RING * i + j, j, c_reg * USES + i, c_reg * T + RING * i + j)

    def copy_banks(eng, copy, e):
        for n, (c0, w) in list(enumerate(CHUNKS))[e::2]:
            eng.wait_ge(turned, n + 1)
            copy(h_t[:, c0:c0 + w], banks[0:D, n, 0:w]).then_inc(h_t_ready[e], 1)
        for n, (c0, w) in list(enumerate(CHUNKS))[e::2]:
            eng.wait_ge(qk_ready, n + 1)
            ins = copy(qk_t[:, c0:c0 + w], banks[:, n, 0:w])
        ins.then_inc(qk_copied[e], 1)

    N_SCORED = -(-N // 64) * 64

    def columns(width):
        return BANK if width == 4 else N_SCORED - SC * BANK

    def over_chunks(eng, chunk):
        with eng.Fori(0, SC) as ci:
            chunk(ci, 4)
        chunk(SC, T - 4 * SC)

    low, high = slice(0, 2), slice(2, 4)
    LOOPED = (T - 2) // RING * RING

    with nc.Block() as block:
        @block.sync
        def _(sp):
            def keep(part_no):
                sp.wait_ge(parts_ready, part_no + 1)
                sp.dma_start(parts_dram[part_no].rearrange("w h d n -> (w h d) n"), part[:, part_no]
                             ).then_inc(parts_stored[part_no], 16)

            def place(part_no):
                sp.wait_ge(parts_stored[part_no], 16)
                for side, to, part_of in ((0, q6, QPART), (1, k6, KPART)):
                    for n in range(NPART):
                        if part_of[n] == part_no:
                            sp.dma_start(to[n * HD:(n + 1) * HD],
                                         parts_dram[part_no, side].rearrange("h d n -> d h n")).then_inc(rows_placed, 16)

            keep(0)
            keep(1)
            place(0)
            keep(2)
            place(1)
            place(2)
            blocks = counts_dram.rearrange("(s p) d -> p s d", p=P)

            def chunk(ci, width):
                def load(t, j, n, u):
                    sp.wait_ge(counts_turned, u + 1)
                    sp.dma_start(count[:, j, 0:width], blocks[:, bass.ds(4 * ci, width), bass.ds(t * P, P)]
                                 ).then_inc(count_landed[j], 16)
                over_tiles(sp, ci, load)

            over_chunks(sp, chunk)
            for f, ts in enumerate(out_parts):
                sp.wait_ge(out_ready, f + 1)
                full = slice(ts.start, min(ts.stop, T - 1))
                sp.dma_start(out[full.start * P:full.stop * P].rearrange("(t p) f -> p t f", p=P), tmp[:, full]
                             ).then_inc(out_stored, 16)
            sp.dma_start(out[(T - 1) * P:N], tmp[0:LAST, T - 1]).then_inc(out_stored, 16)
            sp.wait_ge(out_stored, 48)

        @block.scalar
        def _(act):
            act.wait_ge(var_ready, 1)
            nc.scalar.activation(stat[:, 2], stat[:, 1], ACT.Sqrt).then_inc(std_ready, 1)
            copy_banks(act, nc.scalar.copy, 0)
            act.wait_ge(consts_set, 2)
            nc.scalar.activation(stat[:, 0, 0:1], shift[:, 1:2], ACT.Exp)
            for f in range(2):
                act.sem_inc(scores_read[f], 1)

            def chunk(ci, width):
                W = columns(width)

                def exps(t, j, n, u):
                    act.wait_ge(values_added, u + 1)
                    act.wait_ge(scored[1], u + 1)
                    nc.scalar.activation(att[:, j, high, 0:W], scores[:, high, 0:W], ACT.Relu, bias=shift[:, 0:1]
                                         ).then_inc(scores_read[1], 1)
                    act.wait_ge(scored[0], u + 1)
                    nc.scalar.activation(att[:, j, low, 0:W], scores[:, low, 0:W], ACT.Exp).then_inc(scores_read[0], 1)
                    act.wait_ge(scores_read[1], u + 2)
                    nc.scalar.activation(att[:, j, high, 0:W], att[:, j, high, 0:W], ACT.Exp, bias=shift[:, 1:2]
                                         ).then_inc(expd_high, 1)
                over_tiles(act, ci, exps)

            over_chunks(act, chunk)

        @block.vector
        def _(dve):
            steps = [0]

            def link(ins):
                steps[0] += 1
                ins.then_inc(dve_step, 1)
                dve.wait_ge(dve_step, steps[0])

            layer_norm(nc, dve, link, x, h, tmp, stat, var_ready, std_ready, 0)
            dve.sem_inc(h_ready, 1)
            nc.vector.memset(zero_row[:], 0.0).then_inc(consts_set, 1)
            nc.vector.memset(shift[:, 0:1], CLIP)
            nc.vector.memset(shift[:, 1:2], -CLIP).then_inc(consts_set, 1)
            copy_banks(dve, nc.vector.tensor_copy, 1)
            for e in range(2):
                dve.wait_ge(qk_copied[e], 1)
            for n in range(3):
                nc.vector.tensor_copy(part[:, n], qk_t[:]).then_inc(parts_ready, 1)
                dve.wait_ge(parts_ready, n + 1)
                if n < 2:
                    link(nc.vector.tensor_tensor(qk_t[:], qk_t[:], part[:, n], ALU.subtract))
            dve.wait_ge(v_made, 1)
            dve.wait_ge(v_cleared, 3)
            nc.vector.tensor_copy(v_all[:, :, :, 0:HD],
                                  flat[:, 0:T * D].rearrange("p (t h f) -> p t h f", t=T, h=HEADS)).then_inc(v_copied, 1)
            dve.sem_inc(weighted, 2)
            dve.sem_inc(acc_read, 1)

            def weigher(ci, width):
                W = columns(width)

                def weigh(t, j, n, u):
                    dve.wait_ge(scores_read[0], u + 2)
                    nc.vector.tensor_scalar(att[:, j, low, 0:W], att[:, j, low, 0:W], HI, LO, ALU.min, ALU.max
                                            ).then_inc(clipped, 1)
                    dve.wait_ge(counts_turned, u + RING + 1)
                    dve.wait_ge(expd_high, u + 1)
                    times = count_t[j % 3][:, 0:W].unsqueeze(1).to_broadcast([P, 2, W])
                    nc.vector.scalar_tensor_tensor(att[:, j, high, 0:W], att[:, j, high, 0:W], HI, times,
                                                   ALU.min, ALU.mult)
                    dve.wait_ge(clipped, u + 1)
                    nc.vector.tensor_tensor(att[:, j, low, 0:W], att[:, j, low, 0:W], times, ALU.mult
                                            ).then_inc(weighted, 1)

                def turn(i, first):
                    for j in range(first, RING):
                        weigh(RING * i + j, j, ci * USES + i, ci * T + RING * i + j)

                def read_acc():
                    dve.wait_ge(acc_full, ci + 1)
                    nc.vector.tensor_copy(o_t[:, bass.ds(ci * BANK, W)], acc[:, 0:W]).then_inc(acc_read, 1)

                def first():
                    weigh(0, 0, ci * USES, ci * T)

                def others():
                    turn(0, 1)
                    with dve.Fori(1, USES) as i:
                        turn(i, 0)

                return first, others, read_acc

            def chunk(ci, width, next_width):
                first, others, read_acc = weigher(ci, width)
                others()
                if next_width:
                    weigher(ci + 1, next_width)[0]()
                read_acc()

            weigher(0, 4)[0]()
            with dve.Fori(0, SC - 1) as ci:
                chunk(ci, 4, 4)
            chunk(SC - 1, 4, T - 4 * SC)
            chunk(SC, T - 4 * SC, 0)

            o = flat[:, 0:T * P].rearrange("p (t h f) -> p t h f", t=T, h=HEADS)
            for f, ts in enumerate(out_parts):
                n = ts.stop - ts.start
                dve.wait_ge(nodes_ready, f + 1)
                link(nc.vector.tensor_scalar(den[:, ts], o[:, ts, :, HD], 1e-8, None, ALU.add))
                link(nc.vector.reciprocal(den[:, ts], den[:, ts]))
                link(nc.vector.tensor_tensor(
                    tmp[:, ts].rearrange("p t (h f) -> p (t h) f", h=HEADS),
                    o[:, ts, :, 0:HD].rearrange("p t h f -> p (t h) f"),
                    den[:, ts].rearrange("p t h -> p (t h)").unsqueeze(2).to_broadcast([P, n * HEADS, HD]), ALU.mult))
                nc.vector.tensor_tensor(tmp[:, ts], tmp[:, ts], x[:, ts], ALU.add).then_inc(out_ready, 1)

        @block.gpsimd
        def _(pool):
            nc.gpsimd.memset(o_t[:, N_SCORED:NR], 0.0).then_inc(v_cleared, 1)
            nc.gpsimd.memset(v_all[:], 0.0).then_inc(v_cleared, 1)
            pool.wait_ge(v_cleared, 2)
            nc.gpsimd.memset(v_all[:, :, :, HD:HD + 1], 1.0).then_inc(v_cleared, 1)
            pool.wait_ge(v_copied, 1)

            def chunk(ci, width):
                def take(t, j, n, u):
                    pool.wait_ge(values_added, u + 1)
                    nc.gpsimd.tensor_copy(v_tile[:, j], v_all[:, bass.ds(t, 1)].rearrange("p a h f -> p (a h f)")
                                          ).then_inc(value_taken, 1)
                over_tiles(pool, ci, take)

            over_chunks(pool, chunk)

        @block.tensor
        def _(pe):
            pe.wait_ge(h_ready, 1)
            for c0, w in CHUNKS:
                for t in range(c0 // P, (c0 + w) // P):
                    ins = nc.tensor.transpose(flat[0:D, t * P:(t + 1) * P], h[:, t, :], k["ident"][:])
                ins.then_inc(turned, 1)
            for n, (c0, w) in enumerate(CHUNKS):
                pe.wait_ge(h_t_ready[n % 2], n // 2 + 1)
                nc.tensor.matmul(banks[:, n, 0:w], k["qk"][:], h_t[:, c0:c0 + w], start=True, stop=True
                                 ).then_inc(qk_ready, 1)
            for e in range(2):
                pe.wait_ge(qk_copied[e], 1)
            for t in range(T):
                ins = nc.tensor.matmul(flat[:, t * D:(t + 1) * D], h_t[:, t * P:(t + 1) * P], k["v"][:], start=True,
                                       stop=True, skip_group_check=True)
            ins.then_inc(v_made, 1)
            pe.wait_ge(v_copied, 1)
            pe.wait_ge(consts_set, 2)
            pe.wait_ge(rows_placed, 16 * 2 * NPART)
            pe.sem_inc(counts_turned, RING)
            pe.sem_inc(values_added, RING)

            def steps(ci, width):
                W = columns(width)

                def score(t, j, n, u):
                    for hd in (2, 3, 0, 1):
                        f = hd // 2
                        if hd % 2 == 0:
                            pe.wait_ge(scores_read[f], u + 1)
                        ins = nc.tensor.matmul(scores[:, hd, 0:W], k6[:, hd, bass.ds(t * P, P)],
                                               q6[:, hd, bass.ds(ci * BANK, W)], start=True, stop=True)
                        if hd % 2:
                            ins.then_inc(scored[f], 1)
                    pe.wait_ge(count_landed[j], 16 * n + 16)
                    pe.wait_ge(weighted, u + 1)
                    for s in range(width):
                        ins = nc.tensor.transpose(count_t[j % 3][:, s * P:(s + 1) * P], count[:, j, s, :], k["ident"][:])
                    ins.then_inc(counts_turned, 1)

                def add_values(j, u):
                    pe.wait_ge(value_taken, u + 1)
                    pe.wait_ge(weighted, u + 3)
                    for hd in range(HEADS):
                        ins = nc.tensor.matmul(acc[hd * VW:(hd + 1) * VW, 0:W], v_tile[:, j, hd * VW:(hd + 1) * VW],
                                               att[:, j, hd, 0:W], start=False, stop=True, skip_group_check=True)
                    ins.then_inc(values_added, 1)

                def step(t, j, n):
                    score(t, j, ci * USES + n, ci * T + t)
                    add_values((j - 2) % RING, ci * T + t - 2)

                def scores_of(t):
                    score(t, t, ci * USES, ci * T + t)

                def tiles():
                    pe.wait_ge(acc_read, ci + 1)
                    nc.tensor.matmul(acc[:, 0:W], zero_row[:, 0:P], zero_row[:, 0:W], start=True, stop=False,
                                     skip_group_check=True)
                    with pe.Fori(0, LOOPED // RING) as i:
                        for s in range(RING):
                            step(RING * i + 2 + s, (2 + s) % RING, i + (2 + s) // RING)
                    for t in range(2 + LOOPED, T):
                        step(t, t % RING, t // RING)

                def values_of(t):
                    add_values(t % RING, ci * T + t)

                return scores_of, tiles, values_of

            def chunk(ci, width, next_width):
                scores_of, tiles, values_of = steps(ci, width)
                tiles()
                for n in range(2):
                    if next_width:
                        steps(ci + 1, next_width)[0](n)
                    values_of(T - 2 + n)
                pe.wait_ge(values_added, ci * T + T + RING)
                pe.sem_inc(acc_full, 1)

            for t in range(2):
                steps(0, 4)[0](t)
            with pe.Fori(0, SC - 1) as ci:
                chunk(ci, 4, 4)
            chunk(SC - 1, 4, T - 4 * SC)
            chunk(SC, T - 4 * SC, 0)
            pe.wait_ge(acc_read, SC + 2)
            for ts in out_parts:
                for t in range(ts.start, ts.stop):
                    ins = nc.tensor.transpose(flat[:, t * P:(t + 1) * P], o_t[:, t * P:(t + 1) * P], k["ident"][:])
                ins.then_inc(nodes_ready, 1)


_INS = ["x", "src", "dst", "edge_weight", "L1_gnn_W_self", "L1_gnn_b_self", "L1_gnn_W_neigh", "L1_gnn_b_neigh",
        "L2_gnn_Wxz", "L2_gnn_bxz", "L2_gnn_bhz", "L2_gnn_Wxh", "L2_gnn_bxh", "L2_gnn_bhh",
        "L3_gnn_qTrans", "L3_gnn_kTrans", "L3_gnn_vTrans"]


def kernel(**inputs):
    import numpy as _np
    import concourse.bacc as _bacc
    from concourse import mybir as _mybir
    from concourse.bass_utils import run_bass_kernel_spmd as _run

    nc = _bacc.Bacc("TRN2", target_bir_lowering=False, num_devices=1)
    arrays, args = {}, []
    for name in _INS:
        a = _np.ascontiguousarray(inputs[name])
        arrays[f"in_{name}_dram"] = a
        args.append(nc.dram_tensor(f"in_{name}_dram", a.shape, _mybir.dt.from_np(a.dtype), kind="ExternalInput").ap())
    args.append(nc.dram_tensor("out_0_dram", (N, D), _mybir.dt.float32, kind="ExternalOutput").ap())
    gnn_layers(nc, *args)
    r = _run(nc, [arrays], core_ids=[0])
    return r.results[0]["out_0_dram"]
```
